# Optimizing a Trainium2 kernel written in Bass

```python
import numpy as np
import jax
import jax.numpy as jnp

def _softmax(x, axis=-1):
    return jax.nn.softmax(x, axis=axis)

def _gelu(x):
    return jax.nn.gelu(x, approximate=True)

def _silu(x):
    return jax.nn.silu(x)

def _sigmoid(x):
    return jax.nn.sigmoid(x)

def _layernorm(x, axis=-1, eps=1e-05):
    m = jnp.mean(x, axis=axis, keepdims=True)
    v = jnp.var(x, axis=axis, keepdims=True)
    return (x - m) / jnp.sqrt(v + eps)

def _scatter_add(tgt, idx, src, axis=0):
    return tgt.at[idx].add(src)

def _segment_sum(src, seg, n):
    return jax.ops.segment_sum(src, seg, n)
kernel_name = 'mk_gnn_preln_d4_gnn_r32_350206'

def setup_inputs(seed: int=0):
    np.random.seed(seed)
    _w = jnp.asarray

    def _rec_inputs():
        import jax
        import jax.numpy as jnp
        _gk = jax.random.key(seed)
        x = -0.0003713 + 1 * jax.random.normal(jax.random.fold_in(_gk, 1), (50000, 128), jnp.float32)
        src = jax.random.randint(jax.random.fold_in(_gk, 2), (25000,), 0, 50000, jnp.int32)
        dst = jnp.minimum((50000 * jax.random.uniform(jax.random.fold_in(_gk, 3), (25000,)) ** 2.0).astype(jnp.int32), 49999)
        _o = jnp.argsort(dst, stable=True)
        src = src[_o]
        dst = dst[_o]
        edge_weight = jax.random.uniform(jax.random.fold_in(_gk, 12), (25000,), jnp.float32, 0.0, 0.999998)
        return (x, src, dst, edge_weight)
    x, src, dst, edge_weight = _rec_inputs()

    def _L0_gnn_setup():
        import jax, jax.numpy as jnp
        import numpy as np
        N_NODES = 3125
        IN_CH = 128
        HID_CH = 128
        N_EDGES = 50000
        key = jax.random.key(seed)
        k1, k2, k3, k4, k5 = jax.random.split(key, 5)
        x = jax.random.normal(k1, (N_NODES, IN_CH), dtype=jnp.float32)
        edge_index = jax.random.randint(k2, (2, N_EDGES), 0, N_NODES, dtype=jnp.int64)
        W = jax.random.normal(k3, (IN_CH, HID_CH), dtype=jnp.float32) / np.sqrt(IN_CH)
        b = jnp.zeros((HID_CH,), dtype=jnp.float32)
        prelu_a = jnp.full((HID_CH,), 0.25, dtype=jnp.float32)
        return {'x': x, 'edge_index': edge_index, 'W': W, 'b': b, 'prelu_a': prelu_a}
    _L0_gnn_all = _L0_gnn_setup()
    _L0_gnn_in = {k: v for k, v in _L0_gnn_all.items() if k in ('W', 'b', 'prelu_a')}
    del _L0_gnn_all

    def _L1_gnn_setup():
        import jax, jax.numpy as jnp
        import numpy as np
        N_NODES = 3125
        N_EDGES = 20000
        DIM = 128
        key = jax.random.key(seed)
        k1, k2, k3, k4, k5 = jax.random.split(key, 5)
        x = jax.random.normal(k1, (N_NODES, DIM), dtype=jnp.float32)
        edge_index = jax.random.randint(k2, (2, N_EDGES), 0, N_NODES, dtype=jnp.int64)
        edge_weight = jax.random.uniform(k3, (N_EDGES,), dtype=jnp.float32)
        W = jax.random.normal(k4, (DIM, DIM), dtype=jnp.float32) * (1.0 / np.sqrt(DIM))
        b = jax.random.normal(k5, (DIM,), dtype=jnp.float32) * 0.01
        return {'x': x, 'edge_index': edge_index, 'edge_weight': edge_weight, 'W': W, 'b': b}
    _L1_gnn_all = _L1_gnn_setup()
    _L1_gnn_in = {k: v for k, v in _L1_gnn_all.items() if k in ('W', 'b')}
    del _L1_gnn_all

    def _L2_gnn_setup():
        import jax, jax.numpy as jnp
        import numpy as np
        N, E, IN, OUT, H = (3125, 50000, 128, 128, 4)
        C = OUT // H
        NEG_SLOPE = 0.2
        BN_EPS = 1e-05
        key = jax.random.key(seed)
        k = jax.random.split(key, 6)
        x = jax.random.normal(k[0], (N, IN), dtype=jnp.float32)
        edge_index = jax.random.randint(k[1], (2, E), 0, N, dtype=jnp.int64)
        W = jax.random.normal(k[2], (IN, H * C), dtype=jnp.float32) / np.sqrt(IN)
        att_src = jax.random.normal(k[3], (H, C), dtype=jnp.float32) * 0.1
        att_dst = jax.random.normal(k[4], (H, C), dtype=jnp.float32) * 0.1
        gat_bias = jnp.zeros((H * C,), dtype=jnp.float32)
        bn_gamma = jnp.ones((OUT,), dtype=jnp.float32)
        bn_beta = jnp.zeros((OUT,), dtype=jnp.float32)
        return {'x': x, 'edge_index': edge_index, 'W': W, 'att_src': att_src, 'att_dst': att_dst, 'gat_bias': gat_bias, 'bn_gamma': bn_gamma, 'bn_beta': bn_beta}
    _L2_gnn_all = _L2_gnn_setup()
    _L2_gnn_in = {k: v for k, v in _L2_gnn_all.items() if k in ('W', 'att_src', 'att_dst', 'gat_bias', 'bn_gamma', 'bn_beta')}
    del _L2_gnn_all

    def _L3_gnn_setup():
        import jax, jax.numpy as jnp
        import numpy as np
        N_NODES = 50000
        N_EDGES = 18750
        N_IN = 128
        E_H = 256
        N_H = 256
        N_OUT = 128
        key = jax.random.key(seed)
        ks = jax.random.split(key, 8)
        x = jax.random.normal(ks[0], (N_NODES, N_IN), dtype=jnp.float32)
        edge_index = jax.random.randint(ks[1], (2, N_EDGES), 0, N_NODES, dtype=jnp.int64)
        s = lambda fan_in: 1.0 / np.sqrt(fan_in)
        W_e = jax.random.uniform(ks[2], (2 * N_IN, E_H), jnp.float32, -s(2 * N_IN), s(2 * N_IN))
        b_e = jnp.zeros((E_H,), jnp.float32)
        W_n1 = jax.random.uniform(ks[3], (E_H + N_IN, N_H), jnp.float32, -s(E_H + N_IN), s(E_H + N_IN))
        b_n1 = jnp.zeros((N_H,), jnp.float32)
        W_n2 = jax.random.uniform(ks[4], (N_H, N_OUT), jnp.float32, -s(N_H), s(N_H))
        b_n2 = jnp.zeros((N_OUT,), jnp.float32)
        return {'x': x, 'edge_index': edge_index, 'W_e': W_e, 'b_e': b_e, 'W_n1': W_n1, 'b_n1': b_n1, 'W_n2': W_n2, 'b_n2': b_n2}
    _L3_gnn_all = _L3_gnn_setup()
    _L3_gnn_in = {k: v for k, v in _L3_gnn_all.items() if k in ('W_e', 'b_e', 'W_n1', 'b_n1', 'W_n2', 'b_n2')}
    del _L3_gnn_all
    return {'x': x, 'src': src, 'dst': dst, 'edge_weight': edge_weight, 'L0_gnn_W': _L0_gnn_in['W'], 'L0_gnn_b': _L0_gnn_in['b'], 'L0_gnn_prelu_a': _L0_gnn_in['prelu_a'], 'L1_gnn_W': _L1_gnn_in['W'], 'L1_gnn_b': _L1_gnn_in['b'], 'L2_gnn_W': _L2_gnn_in['W'], 'L2_gnn_att_src': _L2_gnn_in['att_src'], 'L2_gnn_att_dst': _L2_gnn_in['att_dst'], 'L2_gnn_gat_bias': _L2_gnn_in['gat_bias'], 'L2_gnn_bn_gamma': _L2_gnn_in['bn_gamma'], 'L2_gnn_bn_beta': _L2_gnn_in['bn_beta'], 'L3_gnn_W_e': _L3_gnn_in['W_e'], 'L3_gnn_b_e': _L3_gnn_in['b_e'], 'L3_gnn_W_n1': _L3_gnn_in['W_n1'], 'L3_gnn_b_n1': _L3_gnn_in['b_n1'], 'L3_gnn_W_n2': _L3_gnn_in['W_n2'], 'L3_gnn_b_n2': _L3_gnn_in['b_n2']}

def reference(x, src, dst, edge_weight, L0_gnn_W, L0_gnn_b, L0_gnn_prelu_a, L1_gnn_W, L1_gnn_b, L2_gnn_W, L2_gnn_att_src, L2_gnn_att_dst, L2_gnn_gat_bias, L2_gnn_bn_gamma, L2_gnn_bn_beta, L3_gnn_W_e, L3_gnn_b_e, L3_gnn_W_n1, L3_gnn_b_n1, L3_gnn_W_n2, L3_gnn_b_n2):
    import jax
    import jax.numpy as jnp

    def _L0_gnn_ref(x, edge_index, W, b, prelu_a):
        import jax, jax.numpy as jnp
        import numpy as np
        N_NODES = 3125
        IN_CH = 128
        HID_CH = 128
        N_EDGES = 50000
        N = x.shape[0]
        loop = jnp.arange(N, dtype=edge_index.dtype)
        src = jnp.concatenate([edge_index[0], loop])
        dst = jnp.concatenate([edge_index[1], loop])
        deg = jax.ops.segment_sum(jnp.ones_like(dst, dtype=x.dtype), dst, num_segments=N)
        dinv = jnp.where(deg > 0, jax.lax.rsqrt(deg), 0.0)
        norm = dinv[src] * dinv[dst]
        xw = x @ W
        msgs = xw[src] * norm[:, None]
        agg = jax.ops.segment_sum(msgs, dst, num_segments=N) + b
        return jnp.where(agg >= 0, agg, prelu_a * agg)

    def _L1_gnn_ref(x, edge_index, edge_weight, W, b):
        import jax, jax.numpy as jnp
        import numpy as np
        N_NODES = 3125
        N_EDGES = 20000
        DIM = 128
        row, col = (edge_index[0], edge_index[1])
        msgs = edge_weight[:, None] * x[row]
        agg = jax.ops.segment_sum(msgs, col, num_segments=x.shape[0])
        return agg @ W.T + b

    def _L2_gnn_ref(x, edge_index, W, att_src, att_dst, gat_bias, bn_gamma, bn_beta):
        import jax, jax.numpy as jnp
        import numpy as np
        N, E, IN, OUT, H = (3125, 50000, 128, 128, 4)
        C = OUT // H
        NEG_SLOPE = 0.2
        BN_EPS = 1e-05
        n = x.shape[0]
        h = (x @ W).reshape(n, H, C)
        loop = jnp.arange(n, dtype=edge_index.dtype)
        src = jnp.concatenate([edge_index[0], loop])
        dst = jnp.concatenate([edge_index[1], loop])
        a_src = jnp.einsum('nhc,hc->nh', h, att_src)
        a_dst = jnp.einsum('nhc,hc->nh', h, att_dst)
        e = jax.nn.leaky_relu(a_src[src] + a_dst[dst], NEG_SLOPE)
        m = jax.ops.segment_max(e, dst, num_segments=n)
        e = jnp.exp(e - m[dst])
        s = jax.ops.segment_sum(e, dst, num_segments=n)
        alpha = e / (s[dst] + 1e-16)
        msg = h[src] * alpha[:, :, None]
        out = jax.ops.segment_sum(msg, dst, num_segments=n).reshape(n, H * C)
        out = out + gat_bias
        mean = jnp.mean(out, axis=0)
        var = jnp.var(out, axis=0)
        out = bn_gamma * (out - mean) * jax.lax.rsqrt(var + BN_EPS) + bn_beta
        return jax.nn.relu(out + x)

    def _L3_gnn_ref(x, edge_index, W_e, b_e, W_n1, b_n1, W_n2, b_n2):
        import jax, jax.numpy as jnp
        import numpy as np
        N_NODES = 50000
        N_EDGES = 18750
        N_IN = 128
        E_H = 256
        N_H = 256
        N_OUT = 128
        src, dest = (edge_index[0], edge_index[1])
        edge_in = jnp.concatenate([x[src], x[dest]], axis=1)
        edge_attr = jax.nn.relu(edge_in @ W_e + b_e)
        msg = jax.nn.relu(jnp.concatenate([x[dest], edge_attr], axis=1) @ W_n1 + b_n1)
        agg = jax.ops.segment_sum(msg, dest, num_segments=x.shape[0])
        return jax.nn.relu(agg @ W_n2 + b_n2)
    edge_index = jnp.stack([src, dst])
    h = jnp.maximum(_layernorm(x, axis=-1), 0.0)
    x = x + _L0_gnn_ref(h, edge_index, L0_gnn_W, L0_gnn_b, L0_gnn_prelu_a)
    h = jnp.maximum(_layernorm(x, axis=-1), 0.0)
    x = x + _L1_gnn_ref(h, edge_index, edge_weight, L1_gnn_W, L1_gnn_b)
    h = jnp.maximum(_layernorm(x, axis=-1), 0.0)
    x = x + _L2_gnn_ref(h, edge_index, L2_gnn_W, L2_gnn_att_src, L2_gnn_att_dst, L2_gnn_gat_bias, L2_gnn_bn_gamma, L2_gnn_bn_beta)
    h = jnp.maximum(_layernorm(x, axis=-1), 0.0)
    x = x + _L3_gnn_ref(h, edge_index, L3_gnn_W_e, L3_gnn_b_e, L3_gnn_W_n1, L3_gnn_b_n1, L3_gnn_W_n2, L3_gnn_b_n2)
    return x

_drawn_inputs = setup_inputs


def setup_inputs(seed=0):
    import zlib

    import numpy as np

    out = dict(_drawn_inputs(seed))
    spreads = {'L0_gnn_b': (0.0, 0.1),
     'L0_gnn_prelu_a': (0.25, 0.6),
     'L2_gnn_gat_bias': (0.0, 0.8),
     'L2_gnn_bn_gamma': (1.0, 0.2),
     'L2_gnn_bn_beta': (0.0, 0.1),
     'L3_gnn_b_e': (0.0, 0.8),
     'L3_gnn_b_n1': (0.0, 0.567),
     'L3_gnn_b_n2': (0.0, 0.1)}
    factors = {'L1_gnn_b': 7.639, 'L2_gnn_att_dst': 7.491, 'L3_gnn_W_e': 3.762}
    for name, (base, spread) in spreads.items():
        noise = np.random.default_rng([zlib.crc32(name.encode()), seed]).standard_normal(out[name].shape)
        drawn = base * np.exp(spread * noise) if base else spread * noise
        out[name] = jnp.asarray(drawn.astype(out[name].dtype))
    for name, factor in factors.items():
        out[name] = (out[name] * factor).astype(out[name].dtype)
    return out
```

```python
import concourse.bass as bass
from concourse import mybir
from contextlib import ExitStack

F32 = mybir.dt.float32
I32 = mybir.dt.int32
ALU = mybir.AluOpType
ACT = mybir.ActivationFunctionType
AX = mybir.AxisListType

N, D = 50000, 128
E = 25000
H, C = 4, 32
HS = C + 1
GW = H * HS + H
EH = 256
EPT = 125
RW = EPT + 1
NT = E // EPT
HT = NT // 2
GT = 4
NGE = NT // GT
SLOTS = NT * RW
ROWS = N + SLOTS
NF = N // 128
MAIN = 128 * NF
TAIL = N - MAIN
GD = 3
NGD = NF // GD
EPS = 1e-5
BIG = float(1 << 20)
LOW = -1e30


def known(g):
    return isinstance(g, int)


def before(g, n):
    return known(g) and g < n


def there(g, n):
    return not known(g) or 0 <= g < n


def steps(eng, groups, depth, ahead, body, unroll=4):
    head = unroll * (-(-(depth - 1 + unroll) // unroll))
    main = head + unroll * ((groups - 1 - ahead - head) // unroll)
    for t in range(head):
        body(t, t % unroll)
    with eng.Fori(head // unroll, main // unroll) as i:
        for u in range(unroll):
            body(i * unroll + u, u)
    for t in range(main, groups + depth):
        body(t, t % unroll)


def landed(g, s, ring, dmas=1):
    if known(g):
        return 16 * dmas * (g // ring + 1)
    return (g - s) * (16 * dmas // ring) + 16 * dmas


def gate(kp, eng, sem, value):
    eng.wait_ge(sem, value)
    eng.sem_inc(kp.s_gate, 1)


class Mem:

    def __init__(self, nc, ctx, tag):
        self.nc, self.ctx, self.tag = nc, ctx, tag
        self.sems = []

    def sb(self, name, shape, dt=F32):
        return self.ctx.enter_context(self.nc.sbuf_tensor(f"{self.tag}_{name}", shape, dt))

    def ps(self, name, shape):
        return self.ctx.enter_context(self.nc.psum_tensor(f"{self.tag}_ps_{name}", shape, F32))

    def sem(self, name):
        s = self.ctx.enter_context(self.nc.semaphore(f"{self.tag}_{name}"))
        self.sems.append(s)
        return s

    def ring(self, name, n):
        return [self.sem(f"{name}{i}") for i in range(n)]


def clear(nc, m):
    with nc.Block() as block:
        @block.gpsimd
        def _(pool):
            for s in m.sems:
                pool.sem_clear(s)


def main_rows(table, width):
    return table[0:MAIN, 0:width].rearrange("(p r) d -> p r d", p=128)


def state_rows(table):
    return table[N:ROWS, :].rearrange("(k p) d -> p k d", p=RW)


def node_view(table, width, g):
    if known(g) and g == NGD:
        return table[MAIN:N, 0:width].rearrange("(p r) d -> p r d", r=1)
    return main_rows(table, width)[:, bass.ds(g * GD, GD), :]


def node_size(g):
    return (TAIL, 1) if known(g) and g == NGD else (128, GD)


class Keep:

    def __init__(self, m):
        sb = m.sb
        self.ident = sb("ident", [128, 128])
        self.eps = sb("eps", [128, 1])
        self.ones = sb("ones", [128, 128])
        self.zrow = sb("zrow", [1, 256])
        self.drow = sb("drow", [RW, NT * RW])
        self.dcol = sb("dcol", [RW, NT])
        self.lastc = sb("lastc", [RW, NT])
        self.tlastc = sb("tlastc", [RW, NT])
        self.dinvc = sb("dinvc", [RW, NT])
        self.wcol = sb("wcol", [RW, NT])
        self.srci = sb("srci", [RW, NT], I32)
        self.dsti = sb("dsti", [RW, NT], I32)
        self.sidx = sb("sidx", [RW, NT], I32)
        self.idx = sb("idx", [RW, NT], I32)
        self.slotc = sb("slotc", [RW, NT, 2])
        self.redir = sb("redir", [RW, NT, 2])
        self.bslot = sb("bslot", [HT, 2], I32)
        self.w0 = sb("w0", [128, 128])
        self.w1t = sb("w1t", [128, 128])
        self.wg = sb("wg", [128, GW])
        self.b0 = sb("b0", [128, 1])
        self.nb0 = sb("nb0", [128, 1])
        self.na0 = sb("na0", [128, 1])
        self.b1 = sb("b1", [128, GT, 128])
        self.dd = sb("dd", [RW, NT])
        self.dinv2 = sb("dinv2", [RW, NT])
        self.SA = sb("SA", [RW, NT, 2 * H])
        self.bn = sb("bn", [128, 4])
        self.s_drow = m.sem("drow_loaded")
        self.s_gate = m.sem("gate")
        self.s_gathered = m.ring("rows_gathered", 4)
        self.s_scattered = m.ring("rows_scattered", 4)
        self.s_bound = m.sem("bound_gathered")
        self.gathered = [0] * 4
        self.scattered = [0] * 4

    def counts(self, gathers, scatters, ring=4):
        before = list(self.gathered), list(self.scattered)
        for s in range(ring):
            uses = len(range(s, NGE, ring))
            self.gathered[s] += 16 * gathers * uses
            self.scattered[s] += 16 * scatters * uses
        return before


def phase_prep(nc, m, kp, T, a):
    sb, sem = m.sb, m.sem
    s_mem, s_iota, s_id = sem("memset"), sem("iota"), sem("ident")
    s_ld, s_w, s_f = sem("loads"), sem("weights"), sem("dve")
    s_pe, s_act, s_rows = sem("pe"), sem("act"), sem("rows_stored")
    s_rt = sem("rtable_stored")

    Ei = sb("Ei", [HT, 2, RW + 1], I32)
    Si = sb("Si", [HT, 2, RW], I32)
    Wf = sb("Wf", [HT, 2, RW])
    eidi = sb("eidi", [HT, 2, RW + 1], I32)
    sloti = sb("sloti", [HT, 2, RW + 1], I32)
    coli = sb("coli", [RW, NT], I32)
    nidi = sb("nidi", [128, NF + 1], I32)
    RT = sb("RT", [128, NF + 1, 2])
    Df = sb("Df", [HT, 2, RW + 1])
    Sf = sb("Sf", [HT, 2, RW])
    eid = sb("eid", [HT, 2, RW + 1])
    slot = sb("slot", [HT, 2, RW + 1])
    fl = sb("fl", [HT, 2, EPT])
    llf = sb("llf", [HT, 2, RW])
    v = sb("v", [HT, 3, 2, EPT])
    sc = sb("sc", [HT, 3, 2, EPT])
    zs = sb("zs", [HT, EPT])
    zr = sb("zr", [1, NT])
    row = sb("row", [1, 3, NT])
    rex = sb("rex", [1, 3, NT + 1])
    cx = sb("cx", [HT, 3, 2])
    tl = sb("tl", [HT, 2, RW])
    dinv = sb("dinv", [HT, 2, RW])
    sidxf = sb("sidxf", [HT, 2, RW])
    rst = sb("rst", [HT, 2, RW])
    rb = sb("rb", [HT, 2, RW])
    drs = sb("drs", [HT, 2, RW])
    bsf = sb("bsf", [HT, 2])
    tf = sb("tf", [RW, NT])
    w1 = sb("w1", [128, 128])
    atts = sb("atts", [128, 2, 128])
    wtmp = sb("wtmp", [128, 2, 128])
    acol = sb("acol", [128, 1])
    psR = m.ps("psR", [128, 2048])
    psC = m.ps("psC", [128, 2048])

    dst2 = a["dst"].rearrange("(k j) -> k j", j=EPT)
    src2 = a["src"].rearrange("(k j) -> k j", j=EPT)
    ew2 = a["edge_weight"].rearrange("(k j) -> k j", j=EPT)

    def half(t2, b):
        return t2[b * HT:(b + 1) * HT, :]

    block = m.ctx.enter_context(nc.Block())

    @block.gpsimd
    def _(pool):
        pool.memset(Ei[:, :, :], -1).then_inc(s_mem, 1)
        pool.memset(Si[:, :, :], 0).then_inc(s_mem, 1)
        pool.memset(Wf[:, :, :], 0.0).then_inc(s_mem, 1)
        pool.memset(kp.ident[:, :], 0.0).then_inc(s_mem, 1)
        for t, val in ((kp.eps, EPS), (kp.ones, 1.0), (kp.zrow, 0.0), (zs, 0.0), (zr, 0.0)):
            pool.memset(t[:, :], val).then_inc(s_mem, 1)
        pool.memset(RT[:, :, :], 1.0).then_inc(s_mem, 1)
        pool.memset(rex[:, 0, 0:1], 0.0).then_inc(s_mem, 1)
        pool.memset(rex[:, 1:3, NT:NT + 1], BIG).then_inc(s_mem, 1)
        pool.memset(llf[:, :, 0:1], 0.0).then_inc(s_mem, 1)
        pool.memset(tl[:, :, 0:1], 0.0).then_inc(s_mem, 1)
        pool.memset(tl[:, :, EPT:RW], 1.0).then_inc(s_mem, 1)
        pool.memset(dinv[:, :, 0:1], 1.0).then_inc(s_mem, 1)
        pool.memset(sidxf[:, :, 0:1], BIG).then_inc(s_mem, 1)
        pool.memset(rst[:, :, 0:1], 0.0).then_inc(s_mem, 1)
        pool.memset(rb[:, :, EPT:RW], LOW).then_inc(s_mem, 1)
        pool.wait_ge(s_mem, 19)
        pool.affine_select(out=kp.ident[:, :], in_=kp.ident[:, :], compare_op=ALU.not_equal, fill=1.0,
                           base=0, pattern=[[-1, 128]], channel_multiplier=1).then_inc(s_id, 1)
        pool.iota(eidi[:, :, :], [[HT * EPT, 2], [1, RW + 1]], base=-1, channel_multiplier=EPT).then_inc(s_iota, 1)
        pool.iota(sloti[:, :, :], [[HT * RW, 2], [1, RW + 1]], base=N, channel_multiplier=RW).then_inc(s_iota, 1)
        pool.iota(coli[:, :], [[RW, NT]], base=N, channel_multiplier=1).then_inc(s_iota, 1)
        pool.iota(nidi[:, 0:NF], [[1, NF]], base=0, channel_multiplier=NF).then_inc(s_iota, 1)
        pool.iota(nidi[:, NF:NF + 1], [[1, 1]], base=MAIN, channel_multiplier=1).then_inc(s_iota, 1)

    @block.sync
    def _(sp):
        sp.wait_ge(s_mem, 3)
        for b in range(2):
            sp.dma_start(Ei[:, b, 1:RW], half(dst2, b)).then_inc(s_ld, 16)
            sp.dma_start(Si[:, b, 1:RW], half(src2, b)).then_inc(s_ld, 16)
            sp.dma_start(Wf[:, b, 1:RW], half(ew2, b)).then_inc(s_ld, 16)
        sp.dma_start(Ei[1:HT, 0, 0:1], dst2[0:HT - 1, EPT - 1:EPT], allow_slow_non_contiguous=True).then_inc(s_ld, 16)
        sp.dma_start(Ei[:, 1, 0:1], dst2[HT - 1:NT - 1, EPT - 1:EPT], allow_slow_non_contiguous=True).then_inc(s_ld, 16)
        sp.dma_start(Ei[:, 0, RW:RW + 1], dst2[1:HT + 1, 0:1], allow_slow_non_contiguous=True).then_inc(s_ld, 16)
        sp.dma_start(Ei[0:HT - 1, 1, RW:RW + 1], dst2[HT + 1:NT, 0:1], allow_slow_non_contiguous=True).then_inc(s_ld, 16)
        sp.dma_start(kp.w0[:, :], a["L0_gnn_W"]).then_inc(s_w, 16)
        sp.dma_start(w1[:, :], a["L1_gnn_W"]).then_inc(s_w, 16)
        sp.dma_start(wtmp[:, 0, :], a["L2_gnn_W"]).then_inc(s_w, 16)
        sp.dma_start(atts[:, 0, :], a["L2_gnn_att_src"].rearrange("h c -> (h c)").partition_broadcast(128)).then_inc(s_w, 16)
        sp.dma_start(atts[:, 1, :], a["L2_gnn_att_dst"].rearrange("h c -> (h c)").partition_broadcast(128)).then_inc(s_w, 16)
        sp.dma_start(kp.b0[:, :], a["L0_gnn_b"].rearrange("(p a) -> p a", a=1)).then_inc(s_w, 16)
        sp.dma_start(acol[:, :], a["L0_gnn_prelu_a"].rearrange("(p a) -> p a", a=1)).then_inc(s_w, 16)
        for q in range(GT):
            sp.dma_start(kp.b1[:, q, :], a["L1_gnn_b"].partition_broadcast(128)).then_inc(s_w, 16)
        sp.wait_ge(s_f, 13)
        for b in range(2):
            sp.dma_start(half(T["dr"], b), drs[:, b, :]).then_inc(s_rows, 16)
            sp.dma_start(half(T["rst"], b), rst[:, b, :]).then_inc(s_rows, 16)
            sp.dma_start(half(T["rb"], b), rb[:, b, :]).then_inc(s_rows, 16)
        sp.wait_ge(s_rows, 96)
        flat = T["dr"].rearrange("k j -> (k j)")
        for b in range(4):
            w = NT * RW // 4
            sp.dma_start(kp.drow[:, b * w:(b + 1) * w], flat[b * w:(b + 1) * w].partition_broadcast(RW)).then_inc(kp.s_drow, 16)
        sp.wait_ge(s_f, 15)
        sp.dma_start(T["R"][0:MAIN, :].rearrange("(p r) c -> p r c", p=128), RT[:, 0:NF, :]).then_inc(s_rt, 16)
        sp.dma_start(T["R"][MAIN:N, :], RT[0:TAIL, NF, :]).then_inc(s_rt, 16)
        sp.wait_ge(s_rt, 32)

    @block.vector
    def _(dve):
        n = [0]

        def done(ins):
            n[0] += 1
            ins.then_inc(s_f, 1)
            dve.wait_ge(s_f, n[0])

        dve.wait_ge(s_ld, 160)
        dve.wait_ge(s_mem, 19)
        dve.wait_ge(s_iota, 5)
        dve.tensor_copy(Df[:, :, :], Ei[:, :, :])
        dve.tensor_copy(Sf[:, :, :], Si[:, :, :])
        dve.tensor_copy(eid[:, :, :], eidi[:, :, :])
        done(dve.tensor_copy(slot[:, :, :], sloti[:, :, :]))
        dve.tensor_tensor(fl[:, :, :], Df[:, :, 1:RW], Df[:, :, 0:EPT], ALU.not_equal)
        dve.tensor_copy(drs[:, :, 1:RW], Df[:, :, 1:RW])
        dve.tensor_copy(drs[:, :, 0:1], Df[:, :, EPT:RW])
        done(dve.tensor_tensor(llf[:, :, 1:RW], Df[:, :, 1:RW], Df[:, :, 2:RW + 1], ALU.not_equal))
        dve.tensor_tensor(v[:, 0, :, :], fl[:, :, :], eid[:, :, 1:RW], ALU.mult)
        done(dve.tensor_scalar(sc[:, 2, :, :], llf[:, :, 1:RW], -BIG, BIG, ALU.mult, ALU.add))
        dve.tensor_tensor(v[:, 1, :, :], sc[:, 2, :, :], eid[:, :, 1:RW], ALU.add)
        dve.tensor_tensor(v[:, 2, :, :], sc[:, 2, :, :], slot[:, :, 1:RW], ALU.add)
        dve.tensor_copy(tl[:, :, 1:EPT], llf[:, :, 1:EPT])
        done(dve.tensor_tensor(sidxf[:, :, 1:RW], sc[:, 2, :, :], Df[:, :, 1:RW], ALU.add))
        for b in range(2):
            dve.tensor_tensor_scan(sc[:, 0, b, :], zs[:, :], v[:, 0, b, :], 0.0, ALU.add, ALU.max)
            for q in (1, 2):
                ins = dve.tensor_tensor_scan(sc[:, q, b, ::-1], zs[:, :], v[:, q, b, ::-1], BIG, ALU.add, ALU.min)
        done(ins)
        dve.wait_ge(s_pe, 1)
        done(dve.tensor_copy(row[:, :, :], psR[0:1, 0:1536].rearrange("p (a w) -> p a w", a=3)[:, :, 0:NT]))
        dve.tensor_tensor_scan(rex[:, 0, 1:NT + 1], zr[:, :], row[:, 0, :], 0.0, ALU.add, ALU.max)
        dve.tensor_tensor_scan(rex[:, 1, 0:NT][:, ::-1], zr[:, :], row[:, 1, ::-1], BIG, ALU.add, ALU.min)
        done(dve.tensor_tensor_scan(rex[:, 2, 0:NT][:, ::-1], zr[:, :], row[:, 2, ::-1], BIG, ALU.add, ALU.min))
        dve.wait_ge(s_pe, 2)
        done(dve.tensor_copy(cx[:, :, :], psC[0:HT, 0:6].rearrange("p (a b) -> p a b", a=3)))
        for b in range(2):
            dve.tensor_scalar(v[:, 0, b, :], sc[:, 0, b, :], cx[:, 0, b:b + 1], None, ALU.max)
            dve.tensor_scalar(v[:, 1, b, :], sc[:, 1, b, :], cx[:, 1, b:b + 1], None, ALU.min)
            ins = dve.tensor_scalar(bsf[:, b:b + 1], sc[:, 2, b, EPT - 1:EPT], cx[:, 2, b:b + 1], None, ALU.min)
        done(ins)
        dve.tensor_copy(kp.bslot[:, :], bsf[:, :])
        done(dve.tensor_tensor(v[:, 2, :, :], v[:, 1, :, :], v[:, 0, :, :], ALU.subtract))
        done(dve.tensor_scalar(v[:, 2, :, :], v[:, 2, :, :], 2.0, None, ALU.add))
        dve.wait_ge(s_act, 1)
        done(dve.reciprocal(dinv[:, :, 1:RW], v[:, 1, :, :]))
        dve.tensor_scalar(rst[:, :, 1:RW], fl[:, :, :], LOW, None, ALU.mult)
        done(dve.tensor_scalar(rb[:, :, 0:EPT], fl[:, :, :], LOW, None, ALU.mult))
        dve.tensor_copy(RT[:, :, 0], nidi[:, :])
        done(dve.tensor_scalar(tf[:, :], coli[:, :], 1.0, None, ALU.mult))
        done(dve.tensor_copy(kp.slotc[:, :, 0], tf[:, :]))
        dve.wait_ge(s_pe, 3)
        t = psR[0:RW, :].rearrange("p (a w) -> p a w", a=8)[:, :, 0:NT]
        dve.tensor_copy(kp.dcol[:, :], t[:, 0, :])
        dve.tensor_copy(kp.lastc[:, :], t[:, 1, :])
        dve.tensor_copy(kp.tlastc[:, :], t[:, 2, :])
        dve.tensor_copy(kp.sidx[:, :], t[:, 3, :])
        dve.tensor_copy(kp.dinvc[:, :], t[:, 4, :])
        dve.tensor_copy(kp.wcol[:, :], t[:, 5, :])
        dve.tensor_copy(kp.srci[:, :], t[:, 6, :])
        done(dve.tensor_scalar(kp.dsti[:, :], t[:, 0, :], 0.0, None, ALU.max))
        dve.tensor_copy(kp.slotc[:, :, 1], kp.dinvc[:, :])
        dve.wait_ge(s_w, 16 * (7 + GT))
        dve.tensor_copy(kp.w1t[:, :], psC[:, 512:640])
        dve.tensor_scalar(kp.nb0[:, :], kp.b0[:, :], -1.0, None, ALU.mult)
        dve.tensor_scalar(kp.na0[:, :], acol[:, :], -1.0, None, ALU.mult)
        wgh = kp.wg[:, 0:H * HS].rearrange("p (h c) -> p h c", h=H)
        dve.tensor_copy(wgh[:, :, 0:C], wtmp[:, 0, :].rearrange("p (h c) -> p h c", h=H))
        dve.tensor_tensor(wtmp[:, 1, :], wtmp[:, 0, :], atts[:, 1, :], ALU.mult)
        done(dve.tensor_tensor(atts[:, 0, :], wtmp[:, 0, :], atts[:, 0, :], ALU.mult))
        dve.tensor_reduce(wgh[:, :, C], atts[:, 0, :].rearrange("p (h c) -> p h c", h=H), AX.X, ALU.add)
        done(dve.tensor_reduce(kp.wg[:, H * HS:GW], wtmp[:, 1, :].rearrange("p (h c) -> p h c", h=H), AX.X, ALU.add))

    @block.scalar
    def _(act):
        act.wait_ge(s_f, 11)
        act.activation(v[:, 1, :, :], v[:, 2, :, :], ACT.Sqrt).then_inc(s_act, 1)

    @block.tensor
    def _(pe):
        pe.wait_ge(s_f, 5)
        pe.wait_ge(s_id, 1)
        for q in range(3):
            at = EPT - 1 if q == 0 else 0
            for b in range(2):
                ins = pe.transpose(psR[0:1, 512 * q + b * HT:512 * q + (b + 1) * HT], sc[:, q, b, at:at + 1],
                                   kp.ident[0:HT, 0:HT])
        ins.then_inc(s_pe, 1)
        pe.wait_ge(s_f, 7)
        for q in range(3):
            for b in range(2):
                o = b * HT + (1 if q else 0)
                ins = pe.transpose(psC[0:HT, 2 * q + b:2 * q + b + 1], rex[:, q, o:o + HT], kp.ident[0:1, 0:1])
        ins.then_inc(s_pe, 1)
        pe.wait_ge(s_f, 12)
        for q, t in enumerate((Df, llf, tl, sidxf, dinv, Wf, Sf)):
            for b in range(2):
                o = 256 * q + b * HT
                ins = pe.transpose(psR[0:RW, o:o + HT], t[:, b, 0:RW], kp.ident[0:HT, 0:HT])
        pe.wait_ge(s_w, 16 * (7 + GT))
        pe.transpose(psC[:, 512:640], w1[:, :], kp.ident[:, :]).then_inc(s_pe, 1)


def phase_nodes(nc, m, kp, T, a):
    sb, sem = m.sb, m.sem
    X = [sb(f"x{i}", [128, GD, 128]) for i in range(4)]
    X1 = [sb(f"x1_{i}", [128, GD, 128]) for i in range(4)]
    X2 = [sb(f"x2_{i}", [128, GD, 128]) for i in range(4)]
    st = [sb(f"st{i}", [128, GD, 6]) for i in range(2)]
    mv = [[sb(f"mv{w}{i}", [128, GD, 2]) for i in range(4)] for w in range(2)]
    sd = [[sb(f"sd{w}{i}", [128, GD]) for i in range(4)] for w in range(2)]
    rs = [[sb(f"rs{w}{i}", [128, GD]) for i in range(4)] for w in range(2)]
    Z = [[sb(f"z{w}{i}", [128, GD, 128]) for i in range(2)] for w in range(2)]
    HTr = [[sb(f"h{w}{i}", [128, GD, 128]) for i in range(2)] for w in range(2)]
    Rp = [sb(f"rp{i}", [128, GD, 128]) for i in range(2)]
    Qp = [sb(f"qp{i}", [128, GD, 128]) for i in range(2)]
    Pt = [sb(f"pt{i}", [128, GD, 128]) for i in range(2)]
    G = [sb(f"g{i}", [128, GD, GW]) for i in range(2)]
    iring = [sb(f"ir{i}", [RW, GT], I32) for i in range(2)]
    vring = [sb(f"vr{i}", [RW, GT, 2]) for i in range(2)]
    bank = [m.ps(f"b{i}", [128, 512]) for i in range(8)]

    s_x = m.ring("x_loaded", 4)
    s_st, s_mv = [sem("stats0"), sem("stats1")], [sem("meanvar0"), sem("meanvar1")]
    s_sd, s_rs, s_z = [sem("std0"), sem("std1")], [sem("rstd0"), sem("rstd1")], [sem("norm0"), sem("norm1")]
    s_t, s_h = [sem("turned0"), sem("turned1")], [sem("relu0"), sem("relu1")]
    s_y, s_q, s_p, s_b = sem("product"), sem("parts"), sem("prelu"), sem("back")
    s_x1, s_x2, s_g, s_ge = sem("x1"), sem("x2"), sem("g"), sem("g_out")
    s_s1, s_s2, s_sg = m.ring("x1_stored", 4), m.ring("x2_stored", 4), m.ring("g_stored", 2)
    s_ic, s_sc, s_gt, s_rc = sem("idx_copied"), kp.s_scattered, kp.s_gathered, sem("redir_copied")

    def cut(t, g):
        p, n = node_size(g)
        return t[0:p, 0:n, :]

    def pst(b, g, w=128):
        p, n = node_size(g)
        return b[0:p, 0:n * w].rearrange("p (n w) -> p n w", n=n)

    def feat(t, g):
        p, n = node_size(g)
        return t[:, 0:n, 0:p]

    def featps(b, g):
        p, n = node_size(g)
        return b[:, 0:n * p].rearrange("p (n w) -> p n w", n=n)

    kp.counts(GT, GT, ring=2)
    groups = NGD + 1
    block = m.ctx.enter_context(nc.Block())

    @block.sync
    def _(sp):
        def load(g):
            if not there(g, groups):
                return
            if not before(g, 4):
                sp.wait_ge(s_x1, g - 3)
            s = g % 4 if known(g) else slot[0]
            sp.dma_start(cut(X[s], g), node_view(a["x"], 128, g)).then_inc(s_x[s], 16)

        slot = [0]
        load(0)
        load(1)

        def body(t, u):
            slot[0] = (u + 2) % 4
            load(t + 2)
            g, s = t - 2, (u - 2) % 4
            if there(g, groups):
                sp.wait_ge(s_x1, g + 1)
                sp.dma_start(node_view(T["X1"], 128, g), cut(X1[s], g)).then_inc(s_s1[s], 16)
                sp.wait_ge(s_x2, g + 1)
                sp.dma_start(node_view(T["X2"], 128, g), cut(X2[s], g)).then_inc(s_s2[s], 16)
            g, s = t - 3, (u - 3) % 4
            if there(g, groups):
                sp.wait_ge(s_ge, g + 1)
                sp.dma_start(node_view(T["G"], GW, g), cut(G[s % 2], g)).then_inc(s_sg[s % 2], 16)

        steps(sp, groups, 4, 2, body)
        for s in range(4):
            uses = len(range(s, groups, 4))
            sp.wait_ge(s_s1[s], 16 * uses)
            sp.wait_ge(s_s2[s], 16 * uses)
        for s in range(2):
            sp.wait_ge(s_sg[s], 16 * len(range(s, groups, 2)))

    @block.vector
    def _(dve):
        def stats(g, w, x, u):
            p, n = node_size(g)
            for q in range(n):
                ins = dve.bn_stats(st[w][0:p, q, :], x[0:p, q, :])
            ins.then_inc(s_st[w], 1)
            gate(kp, dve, s_st[w], g + 1)
            for q in range(n):
                ins = dve.bn_aggr(mv[w][u][0:p, q, :], st[w][0:p, q, :])
            ins.then_inc(s_mv[w], 1)

        def norm(g, w, x, u):
            p, n = node_size(g)
            dve.wait_ge(s_sd[w], g + 1)
            dve.reciprocal(rs[w][u][0:p, 0:n], sd[w][u][0:p, 0:n]).then_inc(s_rs[w], 1)
            if not before(g, 2):
                dve.wait_ge(s_t[w], g - 1)
            dve.wait_ge(s_rs[w], g + 1)
            for q in range(n):
                ins = dve.tensor_scalar(Z[w][u % 2][0:p, q, :], x[0:p, q, :], mv[w][u][0:p, q, 0:1],
                                        rs[w][u][0:p, q:q + 1], ALU.subtract, ALU.mult)
            ins.then_inc(s_z[w], 1)

        def body(t, u):
            g = t
            if there(g, groups):
                dve.wait_ge(s_x[u], landed(g, u, 4))
                stats(g, 0, X[u], u)
            g, s = t - 2, (u - 2) % 4
            if there(g, groups):
                norm(g, 1, X2[s], s)
            g, s = t - 1, (u - 1) % 4
            if there(g, groups):
                dve.wait_ge(s_q, g + 1)
                if not before(g, 2):
                    dve.wait_ge(s_b, g - 1)
                dve.scalar_tensor_tensor(feat(Pt[s % 2], g), feat(Qp[s % 2], g), kp.na0[:, 0:1], feat(Rp[s % 2], g),
                                         ALU.mult, ALU.add).then_inc(s_p, 1)
            if there(t, groups):
                norm(t, 0, X[u], u)
            if there(g, groups):
                p, n = node_size(g)
                dve.wait_ge(s_b, g + 1)
                if not before(g, 4):
                    dve.wait_ge(s_s1[s], landed(g - 4, s, 4))
                dve.tensor_tensor(cut(X1[s], g), cut(X[s], g), pst(bank[3], g), ALU.add).then_inc(s_x1, 1)
                if not before(g, 4):
                    dve.wait_ge(s_s2[s], landed(g - 4, s, 4))
                dve.wait_ge(s_x1, g + 1)
                dve.tensor_tensor(cut(X2[s], g), cut(X1[s], g), kp.b1[0:p, 0:n, :], ALU.add).then_inc(s_x2, 1)
                dve.wait_ge(s_x2, g + 1)
                stats(g, 1, X2[s], s)

        steps(dve, groups, 4, 2, body)

    @block.scalar
    def _(act):
        def root(g, w, s):
            p, n = node_size(g)
            act.wait_ge(s_mv[w], g + 1)
            act.activation(sd[w][s][0:p, 0:n], mv[w][s][0:p, 0:n, 1], ACT.Sqrt, bias=kp.eps[0:p, 0:1]).then_inc(s_sd[w], 1)

        def relu(g, w, s):
            act.wait_ge(s_t[w], g + 1)
            if w == 0:
                if not before(g, 2):
                    act.wait_ge(s_y, g - 1)
            elif not before(g, 2):
                act.wait_ge(s_g, g - 1)
            act.activation(feat(HTr[w][s % 2], g), featps(bank[4 * w + s % 2], g), ACT.Relu).then_inc(s_h[w], 1)

        def body(t, u):
            if there(t, groups):
                root(t, 0, u)
            g2, s2 = t - 2, (u - 2) % 4
            if there(g2, groups):
                relu(g2, 1, s2)
            if there(t, groups):
                relu(t, 0, u)
            if there(g2, groups):
                act.wait_ge(s_g, g2 + 1)
                if not before(g2, 2):
                    act.wait_ge(s_sg[s2 % 2], landed(g2 - 2, s2 % 2, 2))
                act.activation(cut(G[s2 % 2], g2), pst(bank[6 + s2 % 2], g2, GW), ACT.Copy).then_inc(s_ge, 1)
            if there(t, groups):
                act.wait_ge(s_y, t + 1)
                if not before(t, 2):
                    act.wait_ge(s_p, t - 1)
                act.activation(feat(Rp[u % 2], t), featps(bank[2], t), ACT.Relu, bias=kp.b0[:, 0:1])
                act.activation(feat(Qp[u % 2], t), featps(bank[2], t), ACT.Relu, bias=kp.nb0[:, 0:1], scale=-1.0).then_inc(s_q, 1)
            g1, s1 = t - 1, (u - 1) % 4
            if there(g1, groups):
                root(g1, 1, s1)

        steps(act, groups, 4, 2, body)

    @block.tensor
    def _(pe):
        def turn(g, w, s):
            p, n = node_size(g)
            pe.wait_ge(s_z[w], g + 1)
            if not before(g, 2):
                pe.wait_ge(s_h[w], g - 1)
            o = featps(bank[4 * w + s % 2], g)
            for q in range(n):
                ins = pe.transpose(o[:, q, :], Z[w][s % 2][0:p, q, :], kp.ident[0:p, 0:p])
            ins.then_inc(s_t[w], 1)

        def body(t, u):
            g2, s2 = t - 2, (u - 2) % 4
            if there(g2, groups):
                turn(g2, 1, s2)
            g, s = t - 1, (u - 1) % 4
            if there(g, groups):
                p, n = node_size(g)
                pe.wait_ge(s_p, g + 1)
                if not before(g, 1):
                    pe.wait_ge(s_x1, g)
                o = pst(bank[3], g)
                for q in range(n):
                    ins = pe.transpose(o[:, q, :], Pt[s % 2][:, q, 0:p], kp.ident[:, :])
                ins.then_inc(s_b, 1)
            if there(t, groups):
                turn(t, 0, u)
            if there(g2, groups):
                p, n = node_size(g2)
                pe.wait_ge(s_h[1], g2 + 1)
                if not before(g2, 2):
                    pe.wait_ge(s_ge, g2 - 1)
                o = pst(bank[6 + s2 % 2], g2, GW)
                for q in range(n):
                    ins = pe.matmul(o[:, q, :], HTr[1][s2 % 2][:, q, 0:p], kp.wg[:, :], start=True, stop=True)
                ins.then_inc(s_g, 1)
            if there(t, groups):
                pe.wait_ge(s_h[0], t + 1)
                if not before(t, 1):
                    pe.wait_ge(s_q, t)
                pe.matmul(featps(bank[2], t), kp.w0[:, :], feat(HTr[0][u % 2], t), start=True, stop=True).then_inc(s_y, 1)

        steps(pe, groups, 4, 2, body)

    @block.gpsimd
    def _(pool):
        def scatter(t, u):
            r = u % 2
            if not there(t, NGE):
                return
            if not before(t, 2):
                gate(kp, pool, s_sc[r], landed(t - 2, r, 2, GT))
            pool.tensor_copy(iring[r][:, :], kp.sidx[:, bass.ds(t * GT, GT)])
            pool.tensor_copy(vring[r][:, :, :], kp.slotc[:, bass.ds(t * GT, GT), :]).then_inc(s_ic, 1)
            gate(kp, pool, s_ic, t + 1)
            for q in range(GT):
                pool.indirect_dma_start(T["R"], bass.IndirectOffsetOnAxis(ap=iring[r][:, q:q + 1], axis=0),
                                        vring[r][:, q, :], None, bounds_check=N - 1, oob_is_err=False).then_inc(s_sc[r], 16)

        steps(pool, NGE, 2, 0, scatter, unroll=2)
        for r in range(2):
            pool.wait_ge(s_sc[r], 16 * GT * NGE // 2)

        def gather(t, u):
            r = u % 2
            g, s = t - 1, (u - 1) % 2
            if there(t, NGE):
                if not before(t, 2):
                    gate(kp, pool, s_rc, t - 1)
                pool.tensor_copy(iring[r][:, :], kp.srci[:, bass.ds(t * GT, GT)]).then_inc(s_ic, 1)
                gate(kp, pool, s_ic, NGE + t + 1)
                for q in range(GT):
                    pool.indirect_dma_start(vring[r][:, q, :], None, T["R"],
                                            bass.IndirectOffsetOnAxis(ap=iring[r][:, q:q + 1], axis=0)).then_inc(s_gt[r], 16)
            if there(g, NGE):
                gate(kp, pool, s_gt[s], landed(g, s, 2, GT))
                pool.tensor_copy(kp.redir[:, bass.ds(g * GT, GT), :], vring[s][:, :, :]).then_inc(s_rc, 1)

        steps(pool, NGE, 2, 0, gather, unroll=2)
        pool.wait_ge(s_rc, NGE)


def tile_row(kp, k):
    return kp.drow[:, bass.ds(k * RW, RW)]


def gather_groups(kp, pool, table, rows, idx, s_idx, s_rows, s_free, free):
    def body(t, u):
        if not there(t, NGE):
            return
        gate(kp, pool, s_idx, t + 1)
        if not before(t, 4):
            gate(kp, pool, s_free, free(t))
        for dst, ring, tab in zip(rows, idx, table):
            for q in range(GT):
                pool.indirect_dma_start(dst[u][:, q, :], None, tab,
                                        bass.IndirectOffsetOnAxis(ap=ring[u][:, q:q + 1], axis=0)).then_inc(s_rows[u], 16)

    steps(pool, NGE, 1, 0, body)


def phase_edges0(nc, m, kp, T, a):
    sb, sem = m.sb, m.sem
    Xs = [sb(f"xs{i}", [RW, GT, 128]) for i in range(4)]
    Xd = [sb(f"xd{i}", [RW, GT, 128]) for i in range(4)]
    irs = [sb(f"irs{i}", [RW, GT], I32) for i in range(4)]
    ird = [sb(f"ird{i}", [RW, GT], I32) for i in range(4)]
    st = [sb(f"st{i}", [RW, 2 * GT, 6]) for i in range(2)]
    mv = [sb(f"mv{i}", [RW, 2 * GT, 2]) for i in range(2)]
    sd = [sb(f"sd{i}", [RW, 2 * GT]) for i in range(2)]
    rs = [sb(f"rs{i}", [RW, 2 * GT]) for i in range(2)]
    scl = [sb(f"scl{i}", [RW, GT]) for i in range(2)]
    hs = [sb(f"hs{i}", [RW, GT]) for i in range(2)]
    hb = [sb(f"hb{i}", [RW, GT]) for i in range(2)]
    M = [sb(f"m{i}", [RW, GT, 128]) for i in range(2)]
    S = [sb(f"s{i}", [RW, GT, RW]) for i in range(2)]
    Hd = [sb(f"hd{i}", [RW, GT, 128]) for i in range(2)]
    AT = [sb(f"at{i}", [128, GT, RW]) for i in range(2)]
    Rp = [sb(f"rp{i}", [128, GT, RW]) for i in range(2)]
    Qp = [sb(f"qp{i}", [128, GT, RW]) for i in range(2)]
    Pt = [sb(f"pt{i}", [128, GT, RW]) for i in range(2)]
    X1 = [sb(f"x1{i}", [RW, GT, 128]) for i in range(4)]
    psC = m.ps("carry", [128, 512])
    psA = [m.ps(f"agg{i}", [128, 512]) for i in range(2)]
    psZ = [m.ps(f"z{i}", [128, 512]) for i in range(2)]
    psB = [m.ps(f"back{i}", [128, 512]) for i in range(2)]

    s_idx, s_rows = sem("idx_ready"), kp.s_gathered
    s_st, s_mv, s_sd, s_rs = sem("stats"), sem("meanvar"), sem("std"), sem("rstd")
    s_h, s_hn, s_hd, s_m, s_sc, s_s = sem("self_scale"), sem("self_bias"), sem("self_rows"), sem("messages"), sem("scale"), sem("select")
    s_sc0 = sem("scale_rows")
    s_ci, s_co, s_a, s_at, s_z, s_q, s_p, s_b, s_x1 = (sem("carry_in"), sem("carry_out"), sem("summed"), sem("sum_out"),
        sem("product"), sem("parts"), sem("prelu"), sem("back"), sem("x1"))
    s_s1, s_k = m.ring("x1_stored", 4), sem("constants")

    gathered, _ = kp.counts(2 * GT, 0)
    block = m.ctx.enter_context(nc.Block())

    @block.sync
    def _(sp):
        def body(t, u):
            g, s = t - 3, (u - 3) % 4
            if there(g, NGE):
                sp.wait_ge(s_x1, g + 1)
                sp.dma_start(state_rows(T["X1"])[:, bass.ds(g * GT, GT), :], X1[s][:, :, :]).then_inc(s_s1[s], 16)

        steps(sp, NGE, 4, 0, body)
        for s in range(4):
            sp.wait_ge(s_s1[s], 16 * len(range(s, NGE, 4)))

    @block.gpsimd
    def _(pool):
        gather_groups(kp, pool, (a["x"], a["x"]), (Xs, Xd), (irs, ird), s_idx, s_rows, s_x1, lambda g: g - 3)

    @block.vector
    def _(dve):
        def indices(g, s):
            if there(g, NGE):
                if not before(g, 4):
                    dve.wait_ge(s_rows[s], landed(g - 4, s, 4, 2 * GT) + gathered[s])
                dve.tensor_copy(irs[s][:, :], kp.srci[:, bass.ds(g * GT, GT)])
                dve.tensor_copy(ird[s][:, :], kp.dsti[:, bass.ds(g * GT, GT)]).then_inc(s_idx, 1)

        indices(0, 0)
        indices(1, 1)
        dve.wait_ge(kp.s_drow, 64)
        dve.tensor_copy(kp.idx[:, :], kp.redir[:, :, 0])
        dve.tensor_tensor(kp.dd[:, :], kp.redir[:, :, 1], kp.dinvc[:, :], ALU.mult)
        dve.tensor_tensor(kp.dinv2[:, :], kp.dinvc[:, :], kp.dinvc[:, :], ALU.mult).then_inc(s_k, 1)
        dve.wait_ge(s_k, 1)

        def body(t, u):
            indices(t + 2, (u + 2) % 4)
            g, s, r = t - 2, (u - 2) % 4, u % 2
            if there(g, NGE):
                dve.wait_ge(s_b, g + 1)
                if not before(g, 4):
                    dve.wait_ge(s_s1[s], landed(g - 4, s, 4))
                dve.tensor_tensor(X1[s][:, :, :], Xd[s][:, :, :],
                                  psB[r][0:RW, :].rearrange("p (q d) -> p q d", q=GT), ALU.add).then_inc(s_x1, 1)
            if there(t, NGE):
                dve.wait_ge(s_rows[u], landed(t, u, 4, 2 * GT) + gathered[u])
                for w, x in enumerate((Xs[u], Xd[u])):
                    for q in range(GT):
                        ins = dve.bn_stats(st[r][:, w * GT + q, :], x[:, q, :])
                ins.then_inc(s_st, 1)
                gate(kp, dve, s_st, t + 1)
                for q in range(2 * GT):
                    ins = dve.bn_aggr(mv[r][:, q, :], st[r][:, q, :])
                ins.then_inc(s_mv, 1)
                dve.wait_ge(s_mv, t + 1)
                if not before(t, 2):
                    dve.wait_ge(s_a, t - 1)
                for q in range(GT):
                    ins = dve.tensor_scalar(M[r][:, q, :], Xs[u][:, q, :], mv[r][:, q, 0:1], 0.0, ALU.subtract, ALU.max)
                ins.then_inc(s_m, 1)
            g1, r1 = t - 1, (u - 1) % 2
            if there(g1, NGE):
                dve.wait_ge(s_q, g1 + 1)
                dve.scalar_tensor_tensor(Pt[r1][:, :, :], Qp[r1][:, :, :], kp.na0[:, 0:1], Rp[r1][:, :, :],
                                         ALU.mult, ALU.add).then_inc(s_p, 1)
            if there(t, NGE):
                dve.wait_ge(s_sd, t + 1)
                dve.reciprocal(rs[r][:, :], sd[r][:, :]).then_inc(s_rs, 1)
                dve.wait_ge(s_rs, t + 1)
                cols = bass.ds(t * GT, GT)
                dve.tensor_tensor(hs[r][:, :], rs[r][:, GT:2 * GT], kp.dinv2[:, cols], ALU.mult).then_inc(s_h, 1)
                dve.tensor_tensor(scl[r][:, :], rs[r][:, 0:GT], kp.dd[:, cols], ALU.mult).then_inc(s_sc0, 1)
                dve.wait_ge(s_sc0, t + 1)
                dve.memset(scl[r][0:1, :], 1.0).then_inc(s_sc, 1)
                dve.wait_ge(s_h, t + 1)
                dve.scalar_tensor_tensor(hb[r][:, :], mv[r][:, GT:2 * GT, 0], -1.0, hs[r][:, :], ALU.mult, ALU.mult).then_inc(s_hn, 1)
                dve.wait_ge(s_sc, t + 1)
                for q in range(GT):
                    k = t * GT + q
                    ins = dve.tensor_scalar(S[r][:, q, :], tile_row(kp, k), kp.dcol[:, bass.ds(k, 1)],
                                            scl[r][:, q:q + 1], ALU.is_equal, ALU.mult)
                ins.then_inc(s_s, 1)

        steps(dve, NGE, 3, 2, body)

    @block.scalar
    def _(act):
        def body(t, u):
            r = u % 2
            if not there(t, NGE):
                return
            act.wait_ge(s_mv, t + 1)
            act.activation(sd[r][:, :], mv[r][:, :, 1], ACT.Sqrt, bias=kp.eps[0:RW, 0:1]).then_inc(s_sd, 1)
            act.wait_ge(s_hn, t + 1)
            for q in range(GT):
                ins = act.activation(Hd[r][:, q, :], Xd[u][:, q, :], ACT.Relu, bias=hb[r][:, q:q + 1], scale=hs[r][:, q:q + 1])
            ins.then_inc(s_hd, 1)
            act.wait_ge(s_m, t + 1)
            for q in range(GT):
                if before(t, 1) and q == 0:
                    act.activation(M[r][0:1, q, :], kp.zrow[0:1, 0:128], ACT.Copy).then_inc(s_ci, 1)
                    continue
                act.wait_ge(s_co, t * GT + q)
                o = 128 * ((q + 1) % 2)
                act.activation(M[r][0:1, q, :], psC[0:1, o:o + 128], ACT.Copy).then_inc(s_ci, 1)
            act.wait_ge(s_a, t + 1)
            act.activation(AT[r][:, :, :], psA[r][:, 0:GT * RW].rearrange("p (q e) -> p q e", q=GT), ACT.Copy).then_inc(s_at, 1)
            act.wait_ge(s_z, t + 1)
            z = psZ[r][:, 0:GT * RW].rearrange("p (q e) -> p q e", q=GT)
            if not before(t, 2):
                act.wait_ge(s_p, t - 1)
            act.activation(Rp[r][:, :, :], z, ACT.Relu, bias=kp.b0[:, 0:1])
            act.activation(Qp[r][:, :, :], z, ACT.Relu, bias=kp.nb0[:, 0:1], scale=-1.0).then_inc(s_q, 1)

        steps(act, NGE, 1, 0, body)

    @block.tensor
    def _(pe):
        def body(t, u):
            r = u % 2
            if there(t, NGE):
                pe.wait_ge(s_s, t + 1)
                pe.wait_ge(s_hd, t + 1)
                for q in range(GT):
                    pe.wait_ge(s_ci, t * GT + q + 1)
                    o = 128 * (q % 2)
                    pe.matmul(psC[0:1, o:o + 128], S[r][:, q, 0:1], M[r][:, q, :], start=True, stop=True).then_inc(s_co, 1)
                    ag = psA[r][:, q * RW:(q + 1) * RW]
                    pe.matmul(ag, M[r][:, q, :], S[r][:, q, :], start=True, stop=False)
                    ins = pe.matmul(ag, Hd[r][:, q, :], kp.ident[0:RW, 0:RW], start=False, stop=True)
                ins.then_inc(s_a, 1)
            g, r = t - 1, (u - 1) % 2
            if there(g, NGE):
                pe.wait_ge(s_p, g + 1)
                if not before(g, 2):
                    pe.wait_ge(s_x1, g - 1)
                for q in range(GT):
                    ins = pe.transpose(psB[r][0:RW, q * 128:(q + 1) * 128], Pt[r][:, q, :], kp.ident[:, :])
                ins.then_inc(s_b, 1)
            r = u % 2
            if there(t, NGE):
                pe.wait_ge(s_at, t + 1)
                if not before(t, 2):
                    pe.wait_ge(s_q, t - 1)
                pe.matmul(psZ[r][:, 0:GT * RW].rearrange("p (q e) -> p q e", q=GT), kp.w0[:, :], AT[r][:, :, :],
                          start=True, stop=True).then_inc(s_z, 1)

        steps(pe, NGE, 3, 2, body)


def phase_edges1(nc, m, kp, T, a):
    sb, sem = m.sb, m.sem
    Xs = [sb(f"xs{i}", [RW, GT, 128]) for i in range(4)]
    Xp = [sb(f"xp{i}", [RW, GT, 128]) for i in range(4)]
    irs = [sb(f"irs{i}", [RW, GT], I32) for i in range(4)]
    st = [[sb(f"st{w}{i}", [RW, GT, 6]) for i in range(2)] for w in range(2)]
    mv = [[sb(f"mv{w}{i}", [RW, GT, 2]) for i in range(2)] for w in range(2)]
    sd = [[sb(f"sd{w}{i}", [RW, GT]) for i in range(2)] for w in range(2)]
    rs = [[sb(f"rs{w}{i}", [RW, GT]) for i in range(2)] for w in range(2)]
    scl = [sb(f"scl{i}", [RW, GT]) for i in range(2)]
    M = [sb(f"m{i}", [RW, GT, 128]) for i in range(2)]
    S = [sb(f"s{i}", [RW, GT, RW]) for i in range(2)]
    AT = [sb(f"at{i}", [128, GT, RW]) for i in range(2)]
    X2 = [sb(f"x2{i}", [RW, GT, 128]) for i in range(4)]
    Z = [sb(f"z{i}", [RW, GT, 128]) for i in range(2)]
    HT2 = [sb(f"ht{i}", [128, GT, RW]) for i in range(2)]
    G = [sb(f"g{i}", [RW, GT, GW]) for i in range(4)]
    psC = m.ps("carry", [128, 512])
    psA = m.ps("agg", [128, 512])
    psY = [m.ps(f"y{i}", [128, 512]) for i in range(2)]
    psT = m.ps("turn", [128, 512])
    psG = m.ps("g", [128, 1024])

    s_idx, s_rows, s_xp = sem("idx_ready"), kp.s_gathered, m.ring("state_loaded", 4)
    s_st, s_mv = [sem("stats0"), sem("stats1")], [sem("meanvar0"), sem("meanvar1")]
    s_sd, s_rs = [sem("std0"), sem("std1")], [sem("rstd0"), sem("rstd1")]
    s_m, s_sc0, s_sc, s_s = sem("messages"), sem("scale_rows"), sem("scale"), sem("select")
    s_ci, s_co, s_a, s_at, s_y = sem("carry_in"), sem("carry_out"), sem("summed"), sem("sum_out"), sem("product")
    s_xa, s_x2, s_z2, s_t2, s_h2, s_g, s_ge, s_sa = (sem("x2_part"), sem("x2"), sem("norm"), sem("turned"), sem("relu"),
        sem("g"), sem("g_out"), sem("scores"))
    s_s2, s_sg = m.ring("x2_stored", 4), m.ring("g_stored", 4)

    gathered, _ = kp.counts(GT, 0)
    block = m.ctx.enter_context(nc.Block())

    @block.sync
    def _(sp):
        def load(g, s):
            if there(g, NGE):
                if not before(g, 4):
                    sp.wait_ge(s_xa, g - 3)
                sp.dma_start(Xp[s][:, :, :], state_rows(T["X1"])[:, bass.ds(g * GT, GT), :]).then_inc(s_xp[s], 16)

        def body(t, u):
            load(t, u)
            g, s = t - 3, (u - 3) % 4
            if there(g, NGE):
                sp.wait_ge(s_x2, g + 1)
                sp.dma_start(state_rows(T["X2"])[:, bass.ds(g * GT, GT), :], X2[s][:, :, :]).then_inc(s_s2[s], 16)
                sp.wait_ge(s_ge, g + 1)
                sp.dma_start(state_rows(T["G"])[:, bass.ds(g * GT, GT), :], G[s][:, :, :]).then_inc(s_sg[s], 16)

        steps(sp, NGE, 4, 0, body)
        for s in range(4):
            sp.wait_ge(s_s2[s], 16 * len(range(s, NGE, 4)))
            sp.wait_ge(s_sg[s], 16 * len(range(s, NGE, 4)))

    @block.gpsimd
    def _(pool):
        gather_groups(kp, pool, (T["X1"],), (Xs,), (irs,), s_idx, s_rows, s_m, lambda g: g - 3)

    @block.vector
    def _(dve):
        def indices(g, s):
            if there(g, NGE):
                if not before(g, 4):
                    dve.wait_ge(s_rows[s], landed(g - 4, s, 4, GT) + gathered[s])
                dve.tensor_copy(irs[s][:, :], kp.idx[:, bass.ds(g * GT, GT)]).then_inc(s_idx, 1)

        indices(0, 0)
        indices(1, 1)

        def stats(g, w, x, r):
            for q in range(GT):
                ins = dve.bn_stats(st[w][r][:, q, :], x[:, q, :])
            ins.then_inc(s_st[w], 1)
            gate(kp, dve, s_st[w], g + 1)
            for q in range(GT):
                ins = dve.bn_aggr(mv[w][r][:, q, :], st[w][r][:, q, :])
            ins.then_inc(s_mv[w], 1)

        def body(t, u):
            indices(t + 2, (u + 2) % 4)
            r = u % 2
            g, s = t - 2, (u - 2) % 4
            if there(g, NGE):
                dve.wait_ge(s_y, g + 1)
                dve.wait_ge(s_xp[s], landed(g, s, 4))
                if not before(g, 4):
                    dve.wait_ge(s_s2[s], landed(g - 4, s, 4))
                dve.tensor_tensor(X2[s][:, :, :], Xp[s][:, :, :],
                                  psY[r][0:RW, :].rearrange("p (q d) -> p q d", q=GT), ALU.add).then_inc(s_xa, 1)
            if there(t, NGE):
                dve.wait_ge(s_rows[u], landed(t, u, 4, GT) + gathered[u])
                stats(t, 0, Xs[u], r)
            if there(g, NGE):
                dve.wait_ge(s_xa, g + 1)
                dve.tensor_tensor(X2[s][:, :, :], X2[s][:, :, :], kp.b1[0:RW, :, :], ALU.add).then_inc(s_x2, 1)
            if there(t, NGE):
                dve.wait_ge(s_mv[0], t + 1)
                if not before(t, 2):
                    dve.wait_ge(s_a, t - 1)
                for q in range(GT):
                    ins = dve.tensor_scalar(M[r][:, q, :], Xs[u][:, q, :], mv[0][r][:, q, 0:1], 0.0, ALU.subtract, ALU.max)
                ins.then_inc(s_m, 1)
            if there(g, NGE):
                dve.wait_ge(s_x2, g + 1)
                stats(g, 1, X2[s], r)
            if there(t, NGE):
                dve.wait_ge(s_sd[0], t + 1)
                dve.reciprocal(rs[0][r][:, :], sd[0][r][:, :]).then_inc(s_rs[0], 1)
                dve.wait_ge(s_rs[0], t + 1)
                dve.tensor_tensor(scl[r][:, :], rs[0][r][:, :], kp.wcol[:, bass.ds(t * GT, GT)], ALU.mult).then_inc(s_sc0, 1)
                dve.wait_ge(s_sc0, t + 1)
                dve.memset(scl[r][0:1, :], 1.0).then_inc(s_sc, 1)
                dve.wait_ge(s_sc, t + 1)
                for q in range(GT):
                    k = t * GT + q
                    ins = dve.tensor_scalar(S[r][:, q, :], tile_row(kp, k), kp.dcol[:, bass.ds(k, 1)],
                                            scl[r][:, q:q + 1], ALU.is_equal, ALU.mult)
                ins.then_inc(s_s, 1)
            if there(g, NGE):
                dve.wait_ge(s_sd[1], g + 1)
                dve.reciprocal(rs[1][r][:, :], sd[1][r][:, :]).then_inc(s_rs[1], 1)
                if not before(g, 2):
                    dve.wait_ge(s_t2, g - 1)
                dve.wait_ge(s_rs[1], g + 1)
                for q in range(GT):
                    ins = dve.tensor_scalar(Z[r][:, q, :], X2[s][:, q, :], mv[1][r][:, q, 0:1], rs[1][r][:, q:q + 1],
                                            ALU.subtract, ALU.mult)
                ins.then_inc(s_z2, 1)
            g, s = t - 3, (u - 3) % 4
            if there(g, NGE):
                dve.wait_ge(s_ge, g + 1)
                cols = bass.ds(g * GT, GT)
                dve.tensor_copy(kp.SA[:, cols, 0:H], G[s][:, :, C:H * HS:HS])
                dve.tensor_copy(kp.SA[:, cols, H:2 * H], G[s][:, :, H * HS:GW]).then_inc(s_sa, 1)

        steps(dve, NGE, 4, 2, body)

    @block.scalar
    def _(act):
        def root(g, w, r):
            act.wait_ge(s_mv[w], g + 1)
            act.activation(sd[w][r][:, :], mv[w][r][:, :, 1], ACT.Sqrt, bias=kp.eps[0:RW, 0:1]).then_inc(s_sd[w], 1)

        def body(t, u):
            r = u % 2
            if there(t, NGE):
                root(t, 0, r)
            g, s = t - 2, (u - 2) % 4
            if there(g, NGE):
                root(g, 1, r)
            if there(t, NGE):
                act.wait_ge(s_m, t + 1)
                for q in range(GT):
                    if before(t, 1) and q == 0:
                        act.activation(M[r][0:1, q, :], kp.zrow[0:1, 0:128], ACT.Copy).then_inc(s_ci, 1)
                        continue
                    act.wait_ge(s_co, t * GT + q)
                    o = 128 * ((q + 1) % 2)
                    act.activation(M[r][0:1, q, :], psC[0:1, o:o + 128], ACT.Copy).then_inc(s_ci, 1)
                act.wait_ge(s_a, t + 1)
                act.activation(AT[r][:, :, :], psA[:, 0:GT * RW].rearrange("p (q e) -> p q e", q=GT), ACT.Copy).then_inc(s_at, 1)
            if there(g, NGE):
                act.wait_ge(s_t2, g + 1)
                if not before(g, 2):
                    act.wait_ge(s_g, g - 1)
                act.activation(HT2[r][:, :, :], psT[:, 0:GT * RW].rearrange("p (q e) -> p q e", q=GT), ACT.Relu).then_inc(s_h2, 1)
                act.wait_ge(s_g, g + 1)
                if not before(g, 4):
                    act.wait_ge(s_sg[s], landed(g - 4, s, 4))
                    act.wait_ge(s_sa, g - 3)
                act.activation(G[s][:, :, :].rearrange("p (b q) w -> p b q w", b=2),
                               psG[0:RW, :].rearrange("p (b w) -> p b w", b=2)[:, :, 0:2 * GW].rearrange("p b (q w) -> p b q w", q=2),
                               ACT.Copy).then_inc(s_ge, 1)

        steps(act, NGE, 4, 2, body)

    @block.tensor
    def _(pe):
        def body(t, u):
            r = u % 2
            if there(t, NGE):
                pe.wait_ge(s_s, t + 1)
                if not before(t, 1):
                    pe.wait_ge(s_at, t)
                for q in range(GT):
                    pe.wait_ge(s_ci, t * GT + q + 1)
                    o = 128 * (q % 2)
                    pe.matmul(psC[0:1, o:o + 128], S[r][:, q, 0:1], M[r][:, q, :], start=True, stop=True).then_inc(s_co, 1)
                    ins = pe.matmul(psA[:, q * RW:(q + 1) * RW], M[r][:, q, :], S[r][:, q, :], start=True, stop=True)
                ins.then_inc(s_a, 1)
            g = t - 2
            if there(g, NGE):
                pe.wait_ge(s_z2, g + 1)
                if not before(g, 1):
                    pe.wait_ge(s_h2, g)
                for q in range(GT):
                    ins = pe.transpose(psT[:, q * RW:(q + 1) * RW], Z[r][:, q, :], kp.ident[0:RW, 0:RW])
                ins.then_inc(s_t2, 1)
            if there(t, NGE):
                pe.wait_ge(s_at, t + 1)
                if not before(t, 2):
                    pe.wait_ge(s_xa, t - 1)
                for q in range(GT):
                    ins = pe.matmul(psY[r][0:RW, q * 128:(q + 1) * 128], AT[r][:, q, :], kp.w1t[:, :], start=True, stop=True)
                ins.then_inc(s_y, 1)
            if there(g, NGE):
                pe.wait_ge(s_h2, g + 1)
                if not before(g, 1):
                    pe.wait_ge(s_ge, g)
                for q in range(GT):
                    o = 512 * (q // 2) + GW * (q % 2)
                    ins = pe.matmul(psG[0:RW, o:o + GW], HT2[r][:, q, :], kp.wg[:, :], start=True, stop=True)
                ins.then_inc(s_g, 1)

        steps(pe, NGE, 4, 2, body)


def phase_attend(nc, m, kp, T, a):
    sb, sem = m.sb, m.sem
    W4 = GT * RW
    Gs = [sb(f"gs{i}", [RW, GT, GW]) for i in range(4)]
    Gd = [sb(f"gd{i}", [RW, GT, GW]) for i in range(2)]
    irs = [sb(f"irs{i}", [RW, GT], I32) for i in range(4)]
    lst = [sb(f"last{i}", [RW, GT]) for i in range(4)]
    Fx = [sb(f"fx{i}", [RW, GT, RW]) for i in range(2)]
    S = [sb(f"s{i}", [RW, GT, RW]) for i in range(2)]
    A8 = [sb(f"a8{i}", [RW, GT, 2 * H]) for i in range(2)]
    ain = [sb(f"ain{i}", [RW, GT, H]) for i in range(2)]
    rst = [sb(f"rst{i}", [H, W4]) for i in range(2)]
    rb = [sb(f"rb{i}", [H, W4]) for i in range(2)]
    MF = [sb(f"mf{i}", [H, W4]) for i in range(2)]
    MB = [sb(f"mb{i}", [H, W4]) for i in range(2)]
    Ts = sb("ts", [RW, 3, GT, H])
    Tl = sb("tl", [RW, 3, GT, H])
    Td = [sb(f"td{i}", [RW, 2, GT, H]) for i in range(2)]
    Pe = [sb(f"p{i}", [RW, 2, GT, H]) for i in range(4)]
    M = [sb(f"m{i}", [RW, GT, H, HS]) for i in range(2)]
    U = sb("u", [RW, GT, H, C])
    V = sb("v", [RW, GT, H, C])
    den = sb("den", [RW, GT, H])
    rec = sb("rec", [RW, GT, H])
    O = [sb(f"o{i}", [RW, GT, 128]) for i in range(4)]
    SQ = [sb(f"sq{i}", [RW, GT, 128]) for i in range(2)]
    Bd = sb("bd", [HT, 2, GW])
    B8 = sb("b8", [HT, 2, 2 * H])
    psS = m.ps("scores", [128, 512])
    psX = m.ps("maxima", [128, 512])
    psA = m.ps("turned", [128, 512])
    psO = [m.ps(f"o{i}", [128, 1024]) for i in range(2)]
    psN = m.ps("norm", [128, 512])

    s_bd, s_b8, s_b8s, s_sa, s_sa0 = kp.s_bound, sem("bound_packed"), sem("bound_stored"), sem("bound_loaded"), sem("row0_set")
    s_idx, s_rows, s_gd, s_rr = sem("idx_ready"), kp.s_gathered, m.ring("state_loaded", 2), m.ring("resets_loaded", 2)
    s_fx, s_f, s_a8, s_ain0, s_ain, s_ta = sem("fix"), sem("fixed"), sem("own_scores"), sem("scan_in_rows"), sem("scan_in"), sem("scan_in_turned")
    s_a80 = sem("own_scores_rows")
    s_mf, s_mb, s_tm, s_t0, s_tl, s_td, s_e = (sem("max_forward"), sem("max_back"), sem("max_turned"), sem("sums"),
        sem("leaky"), sem("shifted"), sem("weights"))
    s_one, s_m, s_ci, s_co, s_s = sem("ones"), sem("messages"), sem("carry_in"), sem("carry_out"), sem("select")
    s_u, s_v, s_de, s_re, s_o, s_sq, s_n, s_os = (sem("self_part"), sem("total"), sem("denominator"), sem("reciprocal"),
        sem("out"), sem("squares"), sem("norm_sums"), m.ring("out_stored", 4))
    s_fr, s_ex = sem("reciprocal_out"), sem("leaky_out")
    s_bn = sem("sums_out")

    def ocol(r, q, w=H * HS):
        return 512 * (q // 2) + H * HS * (q % 2)

    gathered, _ = kp.counts(GT, 0)
    block = m.ctx.enter_context(nc.Block())

    @block.sync
    def _(sp):
        sp.wait_ge(s_b8, 1)
        for b in range(2):
            sp.dma_start(T["B8"][b * HT:(b + 1) * HT, :], B8[:, b, :]).then_inc(s_b8s, 16)
        sp.wait_ge(s_b8s, 32)
        sp.wait_ge(s_sa0, 2)
        one = T["B8"].rearrange("(a k) c -> a k c", a=1)
        sp.dma_start(kp.SA[RW - 1:RW, :, :], one).then_inc(s_sa, 16)
        sp.dma_start(kp.SA[0:1, 1:NT, :], one[:, 0:NT - 1, :]).then_inc(s_sa, 16)

        def body(t, u):
            r = u % 2
            if there(t, NGE):
                if not before(t, 2):
                    sp.wait_ge(s_mb, t - 1)
                ks = bass.ds(t * GT, GT)
                for buf, tab in ((rst, "rst"), (rb, "rb")):
                    sp.dma_start(buf[r][:, :].rearrange("h (k j) -> h k j", k=GT), T[tab][ks, :].partition_broadcast(H)).then_inc(s_rr[r], 16)
            g, r = t - 2, u % 2
            if there(g, NGE):
                if not before(g, 2):
                    sp.wait_ge(s_u, g - 1)
                sp.dma_start(Gd[r][:, :, :], state_rows(T["G"])[:, bass.ds(g * GT, GT), :]).then_inc(s_gd[r], 16)
            g, s = t - 4, u
            if there(g, NGE):
                sp.wait_ge(s_o, g + 1)
                sp.dma_start(T["O2"].rearrange("(k p) d -> p k d", p=RW)[:, bass.ds(g * GT, GT), :], O[s][:, :, :]).then_inc(s_os[s], 16)

        steps(sp, NGE, 5, 0, body)
        for s in range(4):
            sp.wait_ge(s_os[s], 16 * len(range(s, NGE, 4)))

    @block.gpsimd
    def _(pool):
        for b in range(2):
            pool.indirect_dma_start(Bd[:, b, :], None, T["G"],
                                    bass.IndirectOffsetOnAxis(ap=kp.bslot[:, b:b + 1], axis=0)).then_inc(s_bd, 16)
        pool.memset(kp.SA[0:1, 0, 0:H], LOW).then_inc(s_sa0, 1)
        pool.memset(kp.SA[0:1, 0, H:2 * H], 0.0).then_inc(s_sa0, 1)
        gather_groups(kp, pool, (T["G"],), (Gs,), (irs,), s_idx, s_rows, s_m, lambda g: g - 3)

    @block.vector
    def _(dve):
        def indices(g, s):
            if there(g, NGE):
                if not before(g, 4):
                    dve.wait_ge(s_rows[s], landed(g - 4, s, 4, GT) + gathered[s])
                dve.tensor_copy(irs[s][:, :], kp.idx[:, bass.ds(g * GT, GT)]).then_inc(s_idx, 1)

        dve.wait_ge(s_bd, 32)
        dve.tensor_copy(B8[:, :, 0:H], Bd[:, :, C:H * HS:HS])
        dve.tensor_copy(B8[:, :, H:2 * H], Bd[:, :, H * HS:GW]).then_inc(s_b8, 1)
        indices(0, 0)
        indices(1, 1)
        dve.wait_ge(s_sa, 32)

        def spread(g, r, q):
            if not there(g, NGE):
                return
            if q == 0 and not before(g, 2):
                dve.wait_ge(s_f, g - 1)
            k = g * GT + q
            ins = dve.tensor_scalar(Fx[r][:, q, :], tile_row(kp, k), kp.dcol[:, bass.ds(k, 1)],
                                    kp.tlastc[:, bass.ds(k, 1)], ALU.is_equal, ALU.mult)
            if q == GT - 1:
                ins.then_inc(s_fx, 1)

        for q in range(GT):
            spread(0, 0, q)

        def body(t, u):
            indices(t + 2, (u + 2) % 4)
            r = u % 2
            g, rc = t - 1, (u - 1) % 2
            if there(g, NGE):
                dve.wait_ge(s_rr[rc], landed(g, rc, 2, 2))
                dve.wait_ge(s_ta, g + 1)
                if before(g, 1):
                    dve.tensor_tensor_scan(MF[rc][:, :], rst[rc][:, :], psA[0:H, 0:W4], LOW, ALU.add, ALU.max).then_inc(s_mf, 1)
                else:
                    if not before(g, 2):
                        dve.wait_ge(s_tm, g - 1)
                    dve.tensor_tensor_scan(MF[rc][:, :], rst[rc][:, :], psA[0:H, 0:W4], MF[1 - rc][:, W4 - 1:W4],
                                           ALU.add, ALU.max).then_inc(s_mf, 1)
                dve.wait_ge(s_mf, g + 1)
                dve.tensor_tensor_scan(MB[rc][:, ::-1], rb[rc][:, ::-1], MF[rc][:, ::-1], LOW, ALU.add, ALU.max).then_inc(s_mb, 1)
            if there(t, NGE):
                dve.wait_ge(s_f, t + 1)
                dve.wait_ge(s_rows[u], landed(t, u, 4, GT) + gathered[u])
                if not before(t, 2):
                    dve.wait_ge(s_t0, t - 1)
                dve.tensor_copy(A8[r][:, :, :], psS[0:RW, 0:GT * 2 * H].rearrange("p (q c) -> p q c", q=GT)).then_inc(s_a80, 1)
                dve.wait_ge(s_a80, t + 1)
                dve.tensor_copy(A8[r][0:1, :, :], kp.SA[0:1, bass.ds(t * GT, GT), :]).then_inc(s_a8, 1)
                dve.wait_ge(s_a8, t + 1)
                dve.tensor_tensor(ain[r][:, :, :], Gs[u][:, :, C:H * HS:HS], A8[r][:, :, 0:H], ALU.max).then_inc(s_ain0, 1)
                dve.wait_ge(s_ain0, t + 1)
                dve.memset(ain[r][0:1, :, :], LOW).then_inc(s_ain, 1)
            g, s = t - 3, (u - 3) % 4
            if there(g, NGE):
                rf = s % 2
                dve.wait_ge(s_gd[rf], landed(g, rf, 2))
                p1 = Pe[s][:, 1, :, :]
                num = psO[rf][0:RW, :].rearrange("p (b w) -> p b w", b=2)[:, :, 0:2 * H * HS].rearrange(
                    "p b (x c) -> p b x c", c=HS)
                gd = Gd[rf][:, :, 0:H * HS].rearrange("p q (h c) -> p q h c", h=H)
                if not before(g, 1):
                    dve.wait_ge(s_v, g)
                for q in range(GT):
                    ins = dve.tensor_tensor(U[:, q, :, :], gd[:, q, :, 0:C],
                                            p1[:, q, :].unsqueeze(2).to_broadcast([RW, H, C]), ALU.mult)
                ins.then_inc(s_u, 1)
                dve.wait_ge(s_co, (g + 1) * GT)
                if not before(g, 1):
                    dve.wait_ge(s_re, g)
                dve.tensor_tensor(den[:, :, :].rearrange("p (b q) h -> p b (q h)", b=2), num[:, :, :, C],
                                  p1.rearrange("p (b q) h -> p b (q h)", b=2), ALU.add).then_inc(s_de, 1)
                dve.wait_ge(s_u, g + 1)
                if not before(g, 1):
                    dve.wait_ge(s_o, g)
                for b in range(2):
                    ins = dve.tensor_tensor(V[:, 2 * b:2 * b + 2, :, :].rearrange("p q h c -> p (q h) c"),
                                            U[:, 2 * b:2 * b + 2, :, :].rearrange("p q h c -> p (q h) c"),
                                            num[:, b, :, 0:C], ALU.add)
                ins.then_inc(s_v, 1)
                dve.wait_ge(s_de, g + 1)
                dve.tensor_scalar(den[:, :, :], den[:, :, :], 1e-16, None, ALU.add).then_inc(s_re, 1)
                dve.wait_ge(s_re, g + 1)
                dve.reciprocal(rec[:, :, :], den[:, :, :]).then_inc(s_fr, 1)
                if not before(g, 4):
                    dve.wait_ge(s_os[s], landed(g - 4, s, 4))
                    dve.wait_ge(s_n, g - 3)
                dve.wait_ge(s_fr, g + 1)
                dve.wait_ge(s_v, g + 1)
                dve.tensor_copy(lst[s][:, :], kp.lastc[:, bass.ds(g * GT, GT)])
                ins = dve.tensor_tensor(O[s][:, :, :].rearrange("p q (h c) -> p (q h) c", h=H),
                                        V[:, :, :, :].rearrange("p q h c -> p (q h) c"),
                                        rec[:, :, :].rearrange("p q h -> p (q h)").unsqueeze(2).to_broadcast([RW, GT * H, C]),
                                        ALU.mult)
                ins.then_inc(s_o, 1)
            g, s = t - 1, (u - 1) % 4
            if there(g, NGE):
                rd = s % 2
                dve.wait_ge(s_tm, g + 1)
                if not before(g, 1):
                    dve.wait_ge(s_tl, g)
                dst_score = A8[rd][:, :, H:2 * H]
                dve.tensor_tensor(Ts[:, 0, :, :], Gs[s][:, :, C:H * HS:HS], dst_score, ALU.add).then_inc(s_tl, 1)
                dve.tensor_tensor(Ts[:, 1, :, :], psX[0:RW, 0:GT * H].rearrange("p (q h) -> p q h", q=GT),
                                  dst_score, ALU.add)
                dve.tensor_tensor(Ts[:, 2, :, :], A8[rd][:, :, 0:H], dst_score, ALU.add)
                dve.wait_ge(s_tl, g + 1)
                dve.tensor_tensor(Ts[0:1, 0, :, :], psX[0:1, 64:64 + GT * H].rearrange("p (q h) -> p q h", q=GT),
                                  A8[rd][0:1, :, H:2 * H], ALU.add).then_inc(s_t0, 1)
                dve.wait_ge(s_t0, g + 1)
                dve.scalar_tensor_tensor(Tl[:, :, :, :], Ts[:, :, :, :], 0.2, Ts[:, :, :, :], ALU.mult, ALU.max).then_inc(s_ex, 1)
                if not before(g, 2):
                    dve.wait_ge(s_e, g - 1)
                dve.wait_ge(s_ex, g + 1)
                for w in range(2):
                    ins = dve.tensor_tensor(Td[rd][:, w, :, :], Tl[:, 2 * w, :, :], Tl[:, 1, :, :], ALU.subtract)
                ins.then_inc(s_td, 1)
            g, s = t - 2, (u - 2) % 4
            if there(g, NGE):
                re = s % 2
                for q in range(GT):
                    k = g * GT + q
                    if q == 0 and not before(g, 2):
                        dve.wait_ge(s_co, (g - 1) * GT)
                    ins = dve.tensor_scalar(S[re][:, q, :], tile_row(kp, k), kp.dcol[:, bass.ds(k, 1)], None, ALU.is_equal)
                ins.then_inc(s_s, 1)
                dve.memset(Gs[s][:, :, C:H * HS:HS], 1.0).then_inc(s_one, 1)
                dve.wait_ge(s_one, g + 1)
                dve.wait_ge(s_e, g + 1)
                p0 = Pe[s][:, 0, :, :]
                for q in range(GT):
                    ins = dve.tensor_tensor(M[re][:, q, :, :], Gs[s][:, q, 0:H * HS].rearrange("p (h c) -> p h c", h=H),
                                            p0[:, q, :].unsqueeze(2).to_broadcast([RW, H, HS]), ALU.mult)
                ins.then_inc(s_m, 1)
                dve.wait_ge(s_m, g + 1)
                for q in range(GT):
                    if before(g, 1) and q == 0:
                        dve.memset(M[re][0:1, q, :, :], 0.0).then_inc(s_ci, 1)
                        spread(t + 1, (u + 1) % 2, q)
                        continue
                    dve.wait_ge(s_co, g * GT + q)
                    rp, qp = (re, q - 1) if q else (1 - re, GT - 1)
                    o = ocol(rp, qp)
                    dve.tensor_tensor(M[re][0:1, q, :, :], psO[rp][0:1, o:o + H * HS].rearrange("p (h c) -> p h c", h=H),
                                      p0[0:1, q, :].unsqueeze(2).to_broadcast([1, H, HS]), ALU.mult).then_inc(s_ci, 1)
                    spread(t + 1, (u + 1) % 2, q)
            else:
                for q in range(GT):
                    spread(t + 1, (u + 1) % 2, q)

        steps(dve, NGE, 4, 2, body)
        dve.wait_ge(s_n, NGE)
        dve.tensor_copy(kp.bn[:, 2:4], psN[:, 0:2]).then_inc(s_bn, 1)

    @block.scalar
    def _(act):
        def body(t, u):
            g, s = t - 1, (u - 1) % 4
            if there(g, NGE):
                act.wait_ge(s_td, g + 1)
                if not before(g, 4):
                    act.wait_ge(s_u, g - 3)
                    act.wait_ge(s_ci, (g - 3) * GT)
                act.activation(Pe[s][:, :, :, :], Td[s % 2][:, :, :, :], ACT.Exp).then_inc(s_e, 1)
            g, s = t - 3, (u - 3) % 4
            if there(g, NGE):
                act.wait_ge(s_o, g + 1)
                if not before(g, 2):
                    act.wait_ge(s_n, g - 1)
                act.activation(SQ[s % 2][:, :, :], O[s][:, :, :], ACT.Square).then_inc(s_sq, 1)

        steps(act, NGE, 4, 0, body)

    @block.tensor
    def _(pe):
        pe.wait_ge(s_sa, 32)

        def body(t, u):
            r = u % 2
            if there(t, NGE):
                pe.wait_ge(s_fx, t + 1)
                if not before(t, 1):
                    pe.wait_ge(s_a80, t)
                for q in range(GT):
                    ins = pe.matmul(psS[0:RW, q * 2 * H:(q + 1) * 2 * H], Fx[r][:, q, :],
                                    kp.SA[:, bass.ds(t * GT + q, 1), :].rearrange("p a c -> p (a c)"), start=True, stop=True)
                ins.then_inc(s_f, 1)
            g, rg = t - 1, (u - 1) % 2
            if there(g, NGE):
                if not before(g, 1):
                    pe.wait_ge(s_t0, g)
                gate(kp, pe, s_mb, g + 1)
                for q in range(GT):
                    pe.transpose(psX[0:RW, q * H:(q + 1) * H], MB[rg][:, q * RW:(q + 1) * RW], kp.ident[0:H, 0:H])
                for q in range(GT):
                    ins = pe.transpose(psX[0:1, 64 + q * H:64 + (q + 1) * H], MF[rg][:, q * RW:q * RW + 1], kp.ident[0:H, 0:H])
                ins.then_inc(s_tm, 1)
            if there(t, NGE):
                pe.wait_ge(s_ain, t + 1)
                if not before(t, 1):
                    pe.wait_ge(s_mf, t)
                for q in range(GT):
                    ins = pe.transpose(psA[0:H, q * RW:(q + 1) * RW], ain[r][:, q, :], kp.ident[0:RW, 0:RW])
                ins.then_inc(s_ta, 1)
            g, rg = t - 2, (u - 2) % 2
            if there(g, NGE):
                pe.wait_ge(s_s, g + 1)
                if not before(g, 2):
                    pe.wait_ge(s_v, g - 1)
                for q in range(GT):
                    pe.wait_ge(s_ci, g * GT + q + 1)
                    o = ocol(rg, q)
                    pe.matmul(psO[rg][0:RW, o:o + H * HS].rearrange("p (h c) -> p h c", h=H), S[rg][:, q, :], M[rg][:, q, :, :],
                              start=True, stop=True).then_inc(s_co, 1)
            g, s = t - 4, u
            if there(g, NGE):
                pe.wait_ge(s_sq, g + 1)
                for q in range(GT):
                    first, final = known(g) and g == 0 and q == 0, known(g) and g == NGE - 1 and q == GT - 1
                    pe.matmul(psN[:, 0:1], O[s][:, q, :], lst[s][:, q:q + 1], start=first, stop=final, skip_group_check=True)
                    ins = pe.matmul(psN[:, 1:2], SQ[s % 2][:, q, :], lst[s][:, q:q + 1], start=False, stop=final,
                                    skip_group_check=True)
                ins.then_inc(s_n, 1)

        steps(pe, NGE, 5, 0, body)


def phase_stats(nc, m, kp, T, a):
    sb, sem = m.sb, m.sem
    G = [sb(f"g{i}", [128, GD, GW]) for i in range(4)]
    SQ = [sb(f"sq{i}", [128, GD, 128]) for i in range(4)]
    GC = [sb(f"gc{i}", [128, GD, 128]) for i in range(4)]
    RT = sb("rt", [128, NF + 1, 2])
    mask = sb("mask", [128, NF + 1])
    psN = [m.ps(f"norm{i}", [128, 512]) for i in range(2)]
    s_g, s_rt, s_mk, s_sq, s_gc, s_n, s_bn = (m.ring("g_loaded", 4), sem("r_loaded"), sem("mask"), sem("squares"),
        sem("packed"), sem("sums"), sem("sums_out"))
    groups = NGD + 1
    block = m.ctx.enter_context(nc.Block())

    @block.sync
    def _(sp):
        sp.dma_start(RT[:, 0:NF, :], T["R"][0:MAIN, :].rearrange("(p r) c -> p r c", p=128)).then_inc(s_rt, 16)
        sp.dma_start(RT[0:TAIL, NF, :], T["R"][MAIN:N, :]).then_inc(s_rt, 16)

        def body(t, u):
            if there(t, groups):
                if not before(t, 4):
                    sp.wait_ge(s_sq, t - 3)
                    sp.wait_ge(s_gc, t - 3)
                p, n = node_size(t)
                sp.dma_start(G[u][0:p, 0:n, :], node_view(T["G"], GW, t)).then_inc(s_g[u], 16)

        steps(sp, groups, 1, 0, body)

    def heads(g, u):
        p, n = node_size(g)
        return G[u][0:p, 0:n, 0:H * HS].rearrange("p n (h c) -> p n h c", h=H)[:, :, :, 0:C]

    def whole(t, g, u):
        p, n = node_size(g)
        return t[u][0:p, 0:n, :].rearrange("p n (h c) -> p n h c", h=H)

    @block.vector
    def _(dve):
        dve.wait_ge(s_rt, 32)
        dve.tensor_scalar(mask[:, 0:NF], RT[:, 0:NF, 0], float(N), None, ALU.is_lt)
        dve.tensor_scalar(mask[0:TAIL, NF:NF + 1], RT[0:TAIL, NF:NF + 1, 0], float(N), None, ALU.is_lt).then_inc(s_mk, 1)

        def body(t, u):
            if there(t, groups):
                dve.wait_ge(s_g[u], landed(t, u, 4))
                if not before(t, 4):
                    dve.wait_ge(s_n, t - 3)
                dve.tensor_copy(whole(GC, t, u), heads(t, u)).then_inc(s_gc, 1)

        steps(dve, groups, 1, 0, body)
        dve.wait_ge(s_n, groups)
        for w in range(2):
            ins = dve.tensor_copy(kp.bn[:, w:w + 1], psN[w][:, 0:1])
        ins.then_inc(s_bn, 1)

    @block.scalar
    def _(act):
        def body(t, u):
            if there(t, groups):
                act.wait_ge(s_g[u], landed(t, u, 4))
                if not before(t, 4):
                    act.wait_ge(s_n, t - 3)
                act.activation(whole(SQ, t, u), heads(t, u), ACT.Square).then_inc(s_sq, 1)

        steps(act, groups, 1, 0, body)

    @block.tensor
    def _(pe):
        pe.wait_ge(s_mk, 1)

        def body(t, u):
            if there(t, groups):
                p, n = node_size(t)
                pe.wait_ge(s_sq, t + 1)
                pe.wait_ge(s_gc, t + 1)
                for q in range(n):
                    first, final = known(t) and t == 0 and q == 0, known(t) and t == groups - 1 and q == n - 1
                    mk = mask[0:p, bass.ds(t * GD + q, 1)]
                    pe.matmul(psN[0][:, 0:1], GC[u][0:p, q, :], mk, start=first, stop=final)
                    ins = pe.matmul(psN[1][:, 0:1], SQ[u][0:p, q, :], mk, start=first, stop=final)
                ins.then_inc(s_n, 1)

        steps(pe, groups, 1, 0, body)


def phase_x3(nc, m, kp, T, a, out):
    sb, sem = m.sb, m.sem
    vec = sb("vec", [128, 16])
    gam = sb("gam", [128, 3])
    ds = sb("ds", [128, 2, 128])
    wd = sb("wd", [128, 128])
    wg2 = sb("wg2", [128, 128])
    Sb = sb("sbc", [128, GT, 128])
    Tb = sb("tbc", [128, GT, 128])
    r2 = sb("r2", [128, GT, 128])
    b2 = sb("b2", [128, GT, 128])
    X2 = [sb(f"x2{i}", [128, GT, 128]) for i in range(4)]
    O2 = [sb(f"o2{i}", [128, GT, 128]) for i in range(4)]
    st = [sb(f"st{i}", [128, GT, 6]) for i in range(2)]
    mv = [sb(f"mv{i}", [128, GT, 2]) for i in range(2)]
    sd = [sb(f"sd{i}", [128, GT]) for i in range(2)]
    rs = [sb(f"rs{i}", [128, GT]) for i in range(2)]
    Z = [sb(f"z{i}", [128, GT, 128]) for i in range(2)]
    HTb = [sb(f"ht{i}", [128, GD, 128]) for i in range(2)]
    V = [sb(f"v{i}", [128, GT, 128]) for i in range(2)]
    X3 = [sb(f"x3{i}", [128, GT, 128]) for i in range(4)]
    OU = [sb(f"ou{i}", [128, GD, 128]) for i in range(4)]
    Bx = sb("bx", [HT, 2, 128])
    psT = [m.ps(f"t{i}", [128, 512]) for i in range(2)]
    psO = [m.ps(f"o{i}", [128, 512]) for i in range(2)]
    psV = m.ps("v", [128, 512])
    psW = m.ps("w", [128, 512])

    s_ld, s_c, s_sq, s_bc = sem("vectors_loaded"), sem("coefficients"), sem("root"), sem("broadcast")
    s_x, s_st, s_mv, s_sd, s_rs, s_z = m.ring("x2_loaded", 4), sem("stats"), sem("meanvar"), sem("std"), sem("rstd"), sem("norm")
    s_t, s_h, s_o, s_x3, s_out = sem("turned"), sem("relu"), sem("product"), sem("x3"), sem("out")
    s_s3, s_so = m.ring("x3_stored", 4), m.ring("out_stored", 4)
    e_x, e_o, e_st, e_mv, e_sd, e_rs, e_z = (m.ring("e_x2_loaded", 4), m.ring("e_o_loaded", 4), sem("e_stats"), sem("e_meanvar"),
        sem("e_std"), sem("e_rstd"), sem("e_norm"))
    e_v0, e_v1, e_v2, e_x3, e_s3 = sem("e_scaled"), sem("e_shifted"), sem("e_sum"), sem("e_x3"), m.ring("e_x3_stored", 4)
    s_bx, s_bxs = kp.s_bound, sem("bound_stored")
    groups = NGD + 1

    block = m.ctx.enter_context(nc.Block())

    def cut(t, g):
        p, n = node_size(g)
        return t[0:p, 0:n, :]

    def erows(tab, g):
        return state_rows(T[tab])[:, bass.ds(g * GT, GT), :]

    def erow2(tab, g):
        return T[tab].rearrange("(k p) d -> p k d", p=RW)[:, bass.ds(g * GT, GT), :]

    @block.sync
    def _(sp):
        for i, name in enumerate(("L2_gnn_bn_gamma", "L2_gnn_bn_beta", "L2_gnn_gat_bias")):
            sp.dma_start(gam[:, i:i + 1], a[name].rearrange("(p a) -> p a", a=1)).then_inc(s_ld, 16)
        for q in range(GT):
            sp.dma_start(b2[:, q, :], a["L3_gnn_b_n2"].partition_broadcast(128)).then_inc(s_ld, 16)

        def load(g, s):
            if there(g, groups):
                if not before(g, 4):
                    sp.wait_ge(s_x3, g - 3)
                sp.dma_start(cut(X2[s], g), node_view(T["X2"], 128, g)).then_inc(s_x[s], 16)

        def body(t, u):
            load(t, u)
            g, s = t - 3, (u - 3) % 4
            if there(g, groups):
                sp.wait_ge(s_x3, g + 1)
                sp.dma_start(node_view(T["X3"], 128, g), cut(X3[s], g)).then_inc(s_s3[s], 16)

        steps(sp, groups, 4, 0, body)

        def ebody(t, u):
            if there(t, NGE):
                if known(t) and t < 4:
                    sp.wait_ge(s_x3, groups)
                if not before(t, 4):
                    sp.wait_ge(e_x3, t - 3)
                sp.dma_start(X2[u][0:RW, :, :], erows("X2", t)).then_inc(e_x[u], 16)
                sp.dma_start(O2[u][0:RW, :, :], erow2("O2", t)).then_inc(e_o[u], 16)
            g, s = t - 2, (u - 2) % 4
            if there(g, NGE):
                sp.wait_ge(e_x3, g + 1)
                sp.dma_start(erows("X3", g), X3[s][0:RW, :, :]).then_inc(e_s3[s], 16)

        steps(sp, NGE, 3, 0, ebody)
        for s in range(4):
            sp.wait_ge(s_s3[s], 16 * len(range(s, groups, 4)))
            sp.wait_ge(s_so[s], 16 * len(range(s, groups, 4)))
            sp.wait_ge(e_s3[s], 16 * len(range(s, NGE, 4)))
        sp.wait_ge(s_bx, 64)
        last = T["X3"][N:ROWS, :].rearrange("(k p) d -> k p d", p=RW)[:, RW - 1, :]
        for b in range(2):
            sp.dma_start(last[b * HT:(b + 1) * HT, :], Bx[:, b, :]).then_inc(s_bxs, 16)
        sp.wait_ge(s_bxs, 32)

    @block.gpsimd
    def _(pool):
        pool.wait_ge(s_c, 12)

        def body(t, u):
            if there(t, groups):
                p, nn = node_size(t)
                pool.wait_ge(s_x3, t + 1)
                if not before(t, 4):
                    pool.wait_ge(s_so[u], landed(t - 4, u, 4))
                pool.tensor_tensor(cut(OU[u], t), cut(X3[u], t), r2[0:p, 0:nn, :], ALU.add).then_inc(s_out, 1)

        steps(pool, groups, 1, 0, body)
        for s in range(4):
            pool.wait_ge(e_s3[s], 16 * len(range(s, NGE, 4)))
        for b in range(2):
            pool.indirect_dma_start(Bx[:, b, :], None, T["X3"],
                                    bass.IndirectOffsetOnAxis(ap=kp.bslot[:, b:b + 1], axis=0)).then_inc(s_bx, 16)

    @block.vector
    def _(dve):
        n = [0]

        def done(ins):
            n[0] += 1
            ins.then_inc(s_c, 1)
            dve.wait_ge(s_c, n[0])

        def v(i, w=1):
            return vec[:, i:i + w]

        done(dve.tensor_tensor(v(10, 2), kp.bn[:, 0:2], kp.bn[:, 2:4], ALU.add))
        done(dve.tensor_scalar(v(0, 2), v(10, 2), 1.0 / N, None, ALU.mult))
        done(dve.tensor_tensor(v(2), v(0), v(0), ALU.mult))
        done(dve.tensor_tensor(v(3), v(1), v(2), ALU.subtract))
        dve.wait_ge(s_sq, 1)
        dve.wait_ge(s_ld, 16 * (3 + GT))
        done(dve.reciprocal(v(5), v(4)))
        dve.tensor_tensor(v(7), v(0), gam[:, 2:3], ALU.add)
        done(dve.tensor_tensor(v(6), v(5), gam[:, 0:1], ALU.mult))
        done(dve.tensor_tensor(v(8), gam[:, 2:3], v(7), ALU.subtract))
        done(dve.tensor_tensor(v(8), v(8), v(6), ALU.mult))
        done(dve.tensor_tensor(v(9), v(8), gam[:, 1:2], ALU.add))
        dve.tensor_scalar(ds[:, 0, :], kp.ident[:, :], v(6), None, ALU.mult)
        done(dve.tensor_scalar(ds[:, 1, :], kp.ident[:, :], v(9), None, ALU.mult))
        dve.wait_ge(s_bc, 1)
        for q in range(GT):
            dve.tensor_copy(Sb[:, q, :], psV[:, 0:128])
            dve.tensor_copy(Tb[:, q, :], psV[:, 128:256])
        dve.tensor_scalar(r2[:, :, :], b2[:, :, :], 0.0, None, ALU.max)
        done(dve.tensor_tensor(wg2[:, :].rearrange("p (h c) -> p h c", h=H),
                               kp.wg[:, 0:H * HS].rearrange("p (h c) -> p h c", h=H)[:, :, 0:C],
                               psV[:, 0:128].rearrange("p (h c) -> p h c", h=H), ALU.mult))
        done(dve.tensor_tensor(wd[:, :], wg2[:, :], kp.ident[:, :], ALU.add))

        def body(t, u):
            g, s, r = t - 2, (u - 2) % 4, u % 2
            if there(g, groups):
                p, nn = node_size(g)
                dve.wait_ge(s_o, g + 1)
                if not before(g, 4):
                    dve.wait_ge(s_s3[s], landed(g - 4, s, 4))
                    dve.wait_ge(s_out, g - 3)
                dve.scalar_tensor_tensor(cut(X3[s], g), psO[r][0:p, 0:nn * 128].rearrange("p (n d) -> p n d", n=nn), 0.0,
                                         cut(X2[s], g), ALU.max, ALU.add).then_inc(s_x3, 1)
            if there(t, groups):
                p, nn = node_size(t)
                dve.wait_ge(s_x[u], landed(t, u, 4))
                for q in range(nn):
                    ins = dve.bn_stats(st[r][0:p, q, :], X2[u][0:p, q, :])
                ins.then_inc(s_st, 1)
                gate(kp, dve, s_st, t + 1)
                for q in range(nn):
                    ins = dve.bn_aggr(mv[r][0:p, q, :], st[r][0:p, q, :])
                ins.then_inc(s_mv, 1)
            if there(t, groups):
                p, nn = node_size(t)
                dve.wait_ge(s_sd, t + 1)
                dve.reciprocal(rs[r][0:p, 0:nn], sd[r][0:p, 0:nn]).then_inc(s_rs, 1)
                if not before(t, 2):
                    dve.wait_ge(s_t, t - 1)
                dve.wait_ge(s_rs, t + 1)
                for q in range(nn):
                    ins = dve.tensor_scalar(Z[r][0:p, q, :], X2[u][0:p, q, :], mv[r][0:p, q, 0:1], rs[r][0:p, q:q + 1],
                                            ALU.subtract, ALU.mult)
                ins.then_inc(s_z, 1)

        steps(dve, groups, 3, 0, body)

        def ebody(t, u):
            r = u % 2
            if there(t, NGE):
                dve.wait_ge(e_x[u], landed(t, u, 4))
                if known(t) and t < 2:
                    dve.wait_ge(s_t, groups)
                for q in range(GT):
                    ins = dve.bn_stats(st[r][0:RW, q, :], X2[u][0:RW, q, :])
                ins.then_inc(e_st, 1)
                gate(kp, dve, e_st, t + 1)
                for q in range(GT):
                    ins = dve.bn_aggr(mv[r][0:RW, q, :], st[r][0:RW, q, :])
                ins.then_inc(e_mv, 1)
                dve.wait_ge(e_o[u], landed(t, u, 4))
                dve.tensor_tensor(V[r][0:RW, :, :], O2[u][0:RW, :, :], Sb[0:RW, :, :], ALU.mult).then_inc(e_v0, 1)
                dve.wait_ge(e_v0, t + 1)
                dve.tensor_tensor(V[r][0:RW, :, :], V[r][0:RW, :, :], Tb[0:RW, :, :], ALU.add).then_inc(e_v1, 1)
                dve.wait_ge(e_sd, t + 1)
                dve.reciprocal(rs[r][0:RW, :], sd[r][0:RW, :]).then_inc(e_rs, 1)
                dve.wait_ge(e_rs, t + 1)
                for q in range(GT):
                    ins = dve.tensor_scalar(Z[r][0:RW, q, :], X2[u][0:RW, q, :], mv[r][0:RW, q, 0:1], rs[r][0:RW, q:q + 1],
                                            ALU.subtract, ALU.mult)
                ins.then_inc(e_z, 1)
                dve.wait_ge(e_z, t + 1)
                dve.wait_ge(e_v1, t + 1)
                dve.scalar_tensor_tensor(V[r][0:RW, :, :], Z[r][0:RW, :, :], 0.0, V[r][0:RW, :, :], ALU.max, ALU.add).then_inc(e_v2, 1)
                if known(t) and t < 4:
                    dve.wait_ge(s_s3[u], 16 * len(range(u, groups, 4)))
                    dve.wait_ge(s_out, groups)
                if not before(t, 4):
                    dve.wait_ge(e_s3[u], landed(t - 4, u, 4))
                dve.wait_ge(e_v2, t + 1)
                dve.scalar_tensor_tensor(X3[u][0:RW, :, :], V[r][0:RW, :, :], 0.0, X2[u][0:RW, :, :], ALU.max, ALU.add).then_inc(e_x3, 1)

        steps(dve, NGE, 1, 0, ebody)

    @block.scalar
    def _(act):
        act.wait_ge(s_c, 4)
        act.activation(vec[:, 4:5], vec[:, 3:4], ACT.Sqrt, bias=kp.eps[:, 0:1]).then_inc(s_sq, 1)

        def body(t, u):
            r = u % 2
            if there(t, groups):
                p, n = node_size(t)
                act.wait_ge(s_mv, t + 1)
                act.activation(sd[r][0:p, 0:n], mv[r][0:p, 0:n, 1], ACT.Sqrt, bias=kp.eps[0:p, 0:1]).then_inc(s_sd, 1)
                act.wait_ge(s_t, t + 1)
                if not before(t, 2):
                    act.wait_ge(s_o, t - 1)
                act.activation(HTb[r][:, 0:n, 0:p], psT[r][:, 0:n * p].rearrange("f (n p) -> f n p", n=n), ACT.Relu).then_inc(s_h, 1)
            g, s = t - 3, (u - 3) % 4
            if there(g, groups):
                act.wait_ge(s_out, g + 1)
                act.dma_start(node_view(out, 128, g), cut(OU[s], g)).then_inc(s_so[s], 16)

        steps(act, groups, 4, 0, body)

        def ebody(t, u):
            r = u % 2
            if there(t, NGE):
                act.wait_ge(e_mv, t + 1)
                act.activation(sd[r][0:RW, :], mv[r][0:RW, :, 1], ACT.Sqrt, bias=kp.eps[0:RW, 0:1]).then_inc(e_sd, 1)

        steps(act, NGE, 1, 0, ebody)

    @block.tensor
    def _(pe):
        pe.wait_ge(s_c, 10)
        pe.matmul(psV[:, 0:256], kp.ones[:, :], ds[:, :, :].rearrange("p a d -> p (a d)"), start=True, stop=True).then_inc(s_bc, 1)
        pe.wait_ge(s_c, 12)

        def body(t, u):
            r = u % 2
            if there(t, groups):
                p, n = node_size(t)
                pe.wait_ge(s_z, t + 1)
                if not before(t, 2):
                    pe.wait_ge(s_h, t - 1)
                for q in range(n):
                    ins = pe.transpose(psT[r][:, q * p:(q + 1) * p], Z[r][0:p, q, :], kp.ident[0:p, 0:p])
                ins.then_inc(s_t, 1)
                pe.wait_ge(s_h, t + 1)
                if not before(t, 2):
                    pe.wait_ge(s_x3, t - 1)
                for q in range(n):
                    o = psO[r][0:p, q * 128:(q + 1) * 128]
                    pe.matmul(o, HTb[r][:, q, 0:p], wd[:, :], start=True, stop=False)
                    ins = pe.matmul(o, kp.ones[0:1, 0:p], Tb[0:1, 0, :], start=False, stop=True)
                ins.then_inc(s_o, 1)

        steps(pe, groups, 1, 0, body)


def phase_mlp(nc, m, kp, T, a, out):
    sb, sem = m.sb, m.sem
    W4 = GT * RW
    Xs = [sb(f"xs{i}", [RW, GT, 128]) for i in range(4)]
    Xd = [sb(f"xd{i}", [RW, GT, 128]) for i in range(4)]
    irs = [sb(f"irs{i}", [RW, GT], I32) for i in range(4)]
    iro = [sb(f"iro{i}", [RW, GT], I32) for i in range(4)]
    st = [sb(f"st{i}", [RW, 2 * GT, 6]) for i in range(2)]
    mv = [sb(f"mv{i}", [RW, 2 * GT, 2]) for i in range(2)]
    sd = [sb(f"sd{i}", [RW, 2 * GT]) for i in range(2)]
    rs = [sb(f"rs{i}", [RW, 2 * GT]) for i in range(2)]
    Z = [sb(f"z{i}", [RW, 2 * GT, 128]) for i in range(2)]
    Fx = [sb(f"fx{i}", [RW, GT, RW]) for i in range(2)]
    S = [sb(f"s{i}", [RW, GT, RW]) for i in range(2)]
    Hb = [sb(f"h{i}", [128, 2, W4]) for i in range(2)]
    Eb = [sb(f"e{i}", [128, 2, W4]) for i in range(2)]
    Mb = [sb(f"mm{i}", [128, 2, W4]) for i in range(2)]
    Y = [sb(f"y{i}", [RW, GT, 128]) for i in range(2)]
    V = [sb(f"v{i}", [RW, GT, 128]) for i in range(2)]
    OU = [sb(f"ou{i}", [RW, GT, 128]) for i in range(4)]
    we = sb("we", [128, 2, EH])
    wn1 = sb("wn1", [128, 3, EH])
    wn2 = sb("wn2", [128, 2, 128])
    be = sb("be", [128, 2])
    bn1 = sb("bn1", [128, 2])
    b2 = sb("b2", [128, GT, 128])
    psH = [m.ps(f"h{i}", [128, 512]) for i in range(2)]
    psE = [m.ps(f"e{i}", [128, 512]) for i in range(2)]
    psM = [m.ps(f"m{i}", [128, 512]) for i in range(2)]
    psY = m.ps("y", [128, 512])
    psR = m.ps("r", [128, 512])

    s_w, s_idx, s_rows, s_xd = sem("weights"), sem("idx_ready"), kp.s_gathered, m.ring("state_loaded", 4)
    s_st, s_mv, s_sd, s_rs, s_z, s_fx, s_s = (sem("stats"), sem("meanvar"), sem("std"), sem("rstd"), sem("norm"), sem("fix"), sem("select"))
    s_t, s_h, s_e, s_er, s_m, s_mr, s_y, s_ye = (sem("turned"), sem("relu"), sem("attr"), sem("attr_relu"), sem("msg"),
        sem("msg_relu"), sem("y"), sem("y_out"))
    s_ci, s_co, s_v, s_o, s_sc, s_io = (sem("carry_in"), sem("carry_out"), sem("biased"), sem("out"), kp.s_scattered, sem("out_idx"))

    gathered, scattered = kp.counts(GT, GT)
    block = m.ctx.enter_context(nc.Block())

    @block.sync
    def _(sp):
        sp.dma_start(we[:, :, :], a["L3_gnn_W_e"].rearrange("(k p) n -> p k n", p=128)).then_inc(s_w, 16)
        sp.dma_start(wn1[:, :, :], a["L3_gnn_W_n1"].rearrange("(k p) n -> p k n", p=128)).then_inc(s_w, 16)
        sp.dma_start(wn2[:, :, :], a["L3_gnn_W_n2"].rearrange("(k p) n -> p k n", p=128)).then_inc(s_w, 16)
        for h in range(2):
            sp.dma_start(be[:, h:h + 1], a["L3_gnn_b_e"][h * 128:(h + 1) * 128].rearrange("(p a) -> p a", a=1)).then_inc(s_w, 16)
            sp.dma_start(bn1[:, h:h + 1], a["L3_gnn_b_n1"][h * 128:(h + 1) * 128].rearrange("(p a) -> p a", a=1)).then_inc(s_w, 16)
        for q in range(GT):
            sp.dma_start(b2[:, q, :], a["L3_gnn_b_n2"].partition_broadcast(128)).then_inc(s_w, 16)

        def body(t, u):
            if there(t, NGE):
                if not before(t, 4):
                    sp.wait_ge(s_o, t - 3)
                sp.dma_start(Xd[u][:, :, :], state_rows(T["X3"])[:, bass.ds(t * GT, GT), :]).then_inc(s_xd[u], 16)

        steps(sp, NGE, 1, 0, body)

    @block.gpsimd
    def _(pool):
        def body(t, u):
            if there(t, NGE):
                gate(kp, pool, s_idx, t + 1)
                if not before(t, 4):
                    gate(kp, pool, s_z, t - 3)
                for q in range(GT):
                    pool.indirect_dma_start(Xs[u][:, q, :], None, T["X3"],
                                            bass.IndirectOffsetOnAxis(ap=irs[u][:, q:q + 1], axis=0)).then_inc(s_rows[u], 16)
            g, s = t - 4, u
            if there(g, NGE):
                gate(kp, pool, s_o, g + 1)
                gate(kp, pool, s_io, g + 1)
                for q in range(GT):
                    pool.indirect_dma_start(out, bass.IndirectOffsetOnAxis(ap=iro[s][:, q:q + 1], axis=0), OU[s][:, q, :], None,
                                            bounds_check=N - 1, oob_is_err=False).then_inc(s_sc[s], 16)

        steps(pool, NGE, 5, 0, body)
        for s in range(4):
            pool.wait_ge(s_sc[s], 16 * GT * len(range(s, NGE, 4)) + scattered[s])

    @block.vector
    def _(dve):
        def indices(g, s):
            if there(g, NGE):
                if not before(g, 4):
                    dve.wait_ge(s_rows[s], landed(g - 4, s, 4, GT) + gathered[s])
                dve.tensor_copy(irs[s][:, :], kp.idx[:, bass.ds(g * GT, GT)]).then_inc(s_idx, 1)

        indices(0, 0)
        indices(1, 1)
        dve.wait_ge(s_w, 16 * (7 + GT))

        def body(t, u):
            indices(t + 2, (u + 2) % 4)
            r = u % 2
            if there(t, NGE):
                dve.wait_ge(s_rows[u], landed(t, u, 4, GT) + gathered[u])
                dve.wait_ge(s_xd[u], landed(t, u, 4))
                for w, x in enumerate((Xs[u], Xd[u])):
                    for q in range(GT):
                        ins = dve.bn_stats(st[r][:, w * GT + q, :], x[:, q, :])
                ins.then_inc(s_st, 1)
                gate(kp, dve, s_st, t + 1)
                for q in range(2 * GT):
                    ins = dve.bn_aggr(mv[r][:, q, :], st[r][:, q, :])
                ins.then_inc(s_mv, 1)
                if not before(t, 2):
                    dve.wait_ge(s_t, t - 1)
                for q in range(GT):
                    k = t * GT + q
                    ins = dve.tensor_scalar(Fx[r][:, q, :], tile_row(kp, k), kp.dcol[:, bass.ds(k, 1)],
                                            kp.tlastc[:, bass.ds(k, 1)], ALU.is_equal, ALU.mult)
                ins.then_inc(s_fx, 1)
            g, r1 = t - 1, (u - 1) % 2
            if there(g, NGE):
                if not before(g, 2):
                    dve.wait_ge(s_co, (g - 1) * GT)
                for q in range(GT):
                    k = g * GT + q
                    ins = dve.tensor_scalar(S[r1][:, q, :], tile_row(kp, k), kp.dcol[:, bass.ds(k, 1)], None, ALU.is_equal)
                ins.then_inc(s_s, 1)
            g, s = t - 3, (u - 3) % 4
            if there(g, NGE):
                r3 = s % 2
                dve.wait_ge(s_co, (g + 1) * GT)
                if there(g + 1, NGE):
                    dve.wait_ge(s_ci, (g + 1) * GT + 1)
                dve.tensor_tensor(V[r3][:, :, :], psR[0:RW, :].rearrange("p (q d) -> p q d", q=GT), b2[0:RW, :, :], ALU.add).then_inc(s_v, 1)
                if not before(g, 4):
                    dve.wait_ge(s_sc[s], landed(g - 4, s, 4, GT) + scattered[s])
                dve.tensor_copy(iro[s][:, :], kp.sidx[:, bass.ds(g * GT, GT)]).then_inc(s_io, 1)
                dve.wait_ge(s_v, g + 1)
                dve.scalar_tensor_tensor(OU[s][:, :, :], V[r3][:, :, :], 0.0, Xd[s][:, :, :], ALU.max, ALU.add).then_inc(s_o, 1)
            if there(t, NGE):
                dve.wait_ge(s_sd, t + 1)
                dve.reciprocal(rs[r][:, :], sd[r][:, :]).then_inc(s_rs, 1)
                dve.wait_ge(s_rs, t + 1)
                for w, x in enumerate((Xs[u], Xd[u])):
                    for q in range(GT):
                        i = w * GT + q
                        ins = dve.tensor_scalar(Z[r][:, i, :], x[:, q, :], mv[r][:, i, 0:1], rs[r][:, i:i + 1], ALU.subtract, ALU.mult)
                ins.then_inc(s_z, 1)

        steps(dve, NGE, 4, 2, body)

    @block.scalar
    def _(act):
        act.wait_ge(s_w, 16 * (7 + GT))

        def body(t, u):
            r = u % 2
            g1, r1 = t - 1, (u - 1) % 2
            g2, r2 = t - 2, (u - 2) % 2
            carry(g2, r2, 0)
            if there(t, NGE):
                act.wait_ge(s_mv, t + 1)
                act.activation(sd[r][:, :], mv[r][:, :, 1], ACT.Sqrt, bias=kp.eps[0:RW, 0:1]).then_inc(s_sd, 1)
            for h in range(2):
                if there(g1, NGE):
                    act.wait_ge(s_e, 2 * g1 + h + 1)
                    act.activation(Eb[r1][:, h, :], psE[h][:, 0:W4], ACT.Relu, bias=be[:, h:h + 1]).then_inc(s_er, 1)
                carry(g2, r2, h + 1)
            if there(t, NGE):
                act.wait_ge(s_t, t + 1)
                if not before(t, 2):
                    act.wait_ge(s_m, 2 * (t - 1))
                for w in range(2):
                    ins = act.activation(Hb[r][:, w, :], psH[w][:, 0:W4], ACT.Relu)
                ins.then_inc(s_h, 1)
            carry(g2, r2, 3)
            if there(g1, NGE):
                for h in range(2):
                    act.wait_ge(s_m, 2 * g1 + h + 1)
                    act.activation(Mb[r1][:, h, :], psM[h][:, 0:W4], ACT.Relu, bias=bn1[:, h:h + 1]).then_inc(s_mr, 1)
                act.wait_ge(s_y, g1 + 1)
                act.activation(Y[r1][:, :, :], psY[0:RW, :].rearrange("p (q d) -> p q d", q=GT), ACT.Copy).then_inc(s_ye, 1)

        def carry(g, r, q):
            if not there(g, NGE):
                return
            if q == 0:
                act.wait_ge(s_ye, g + 1)
            if before(g, 1) and q == 0:
                act.activation(Y[r][0:1, q, :], kp.zrow[0:1, 0:128], ACT.Copy).then_inc(s_ci, 1)
                return
            act.wait_ge(s_co, g * GT + q)
            o = 128 * ((q + GT - 1) % GT)
            act.activation(Y[r][0:1, q, :], psR[0:1, o:o + 128], ACT.Copy).then_inc(s_ci, 1)

        steps(act, NGE, 3, 0, body)

    @block.tensor
    def _(pe):
        pe.wait_ge(s_w, 16 * (7 + GT))

        def body(t, u):
            r = u % 2
            g1, r1 = t - 1, (u - 1) % 2
            g2, r2 = t - 2, (u - 2) % 2

            def sums(q):
                if not there(g2, NGE):
                    return
                if q == 0:
                    pe.wait_ge(s_s, g2 + 1)
                    if not before(g2, 1):
                        pe.wait_ge(s_v, g2)
                pe.wait_ge(s_ci, g2 * GT + q + 1)
                pe.matmul(psR[0:RW, q * 128:(q + 1) * 128], S[r2][:, q, :], Y[r2][:, q, :], start=True, stop=True).then_inc(s_co, 1)

            if there(g1, NGE):
                for h in range(2):
                    if h == 0:
                        pe.wait_ge(s_h, g1 + 1)
                    if not before(g1, 1):
                        pe.wait_ge(s_er, 2 * (g1 - 1) + h + 1)
                    for w in range(2):
                        ins = pe.matmul(psE[h][:, 0:W4], we[:, w, h * 128:(h + 1) * 128], Hb[r1][:, w, :], start=(w == 0), stop=(w == 1))
                    ins.then_inc(s_e, 1)
                    sums(h)
            else:
                sums(0)
                sums(1)
            if there(t, NGE):
                pe.wait_ge(s_z, t + 1)
                pe.wait_ge(s_fx, t + 1)
                if not before(t, 1):
                    pe.wait_ge(s_h, t)
                for q in range(GT):
                    pe.transpose(psH[0][:, q * RW:(q + 1) * RW], Z[r][:, q, :], kp.ident[0:RW, 0:RW])
                    ins = pe.matmul(psH[1][:, q * RW:(q + 1) * RW], Z[r][:, GT + q, :], Fx[r][:, q, :], start=True, stop=True)
                ins.then_inc(s_t, 1)
            sums(2)
            if there(g1, NGE):
                for h in range(2):
                    if not before(g1, 1):
                        pe.wait_ge(s_mr, 2 * (g1 - 1) + h + 1)
                    if h == 0:
                        pe.wait_ge(s_er, 2 * g1 + 2)
                    for w in range(3):
                        x = Hb[r1][:, 1, :] if w == 0 else Eb[r1][:, w - 1, :]
                        ins = pe.matmul(psM[h][:, 0:W4], wn1[:, w, h * 128:(h + 1) * 128], x, start=(w == 0), stop=(w == 2))
                    ins.then_inc(s_m, 1)
                    if h == 0:
                        sums(3)
                pe.wait_ge(s_mr, 2 * g1 + 2)
                if not before(g1, 1):
                    pe.wait_ge(s_ye, g1)
                for q in range(GT):
                    for w in range(2):
                        ins = pe.matmul(psY[0:RW, q * 128:(q + 1) * 128], Mb[r1][:, w, q * RW:(q + 1) * RW], wn2[:, w, :],
                                        start=(w == 0), stop=(w == 1))
                ins.then_inc(s_y, 1)
            else:
                sums(3)

        steps(pe, NGE, 3, 0, body)


INPUTS = ["x", "src", "dst", "edge_weight", "L0_gnn_W", "L0_gnn_b", "L0_gnn_prelu_a", "L1_gnn_W", "L1_gnn_b",
          "L2_gnn_W", "L2_gnn_att_src", "L2_gnn_att_dst", "L2_gnn_gat_bias", "L2_gnn_bn_gamma", "L2_gnn_bn_beta",
          "L3_gnn_W_e", "L3_gnn_b_e", "L3_gnn_W_n1", "L3_gnn_b_n1", "L3_gnn_W_n2", "L3_gnn_b_n2"]


def gnn_kernel(nc, a, out):
    T = {name: nc.dram_tensor(f"t_{name}", shape, F32, kind="Internal").ap() for name, shape in (
        ("R", (N, 2)), ("X1", (ROWS, D)), ("X2", (ROWS, D)), ("G", (ROWS, GW)), ("X3", (ROWS, D)),
        ("O2", (SLOTS, D)), ("dr", (NT, RW)), ("rst", (NT, RW)), ("rb", (NT, RW)), ("B8", (NT, 8)))}
    with ExitStack() as whole:
        mk = Mem(nc, whole, "k")
        kp = Keep(mk)
        for phase in PHASES:
            with ExitStack() as ctx:
                m = Mem(nc, ctx, phase.__name__[6:])
                phase(nc, m, kp, T, a) if phase not in WITH_OUT else phase(nc, m, kp, T, a, out)
            clear(nc, m)


PHASES = [phase_prep, phase_nodes, phase_edges0, phase_edges1, phase_attend, phase_stats, phase_x3, phase_mlp]
WITH_OUT = [phase_x3, phase_mlp]


def kernel(**inputs):
    import numpy as _np
    import concourse.bacc as _bacc
    from concourse.bass_utils import run_bass_kernel_spmd as _run

    nc = _bacc.Bacc("TRN2", target_bir_lowering=False, num_devices=1)
    arrays, a = {}, {}
    for name in INPUTS:
        x = _np.ascontiguousarray(inputs[name])
        arrays[f"in_{name}_dram"] = x
        a[name] = nc.dram_tensor(f"in_{name}_dram", x.shape, mybir.dt.from_np(x.dtype), kind="ExternalInput").ap()
    out = nc.dram_tensor("out_0_dram", (N, D), F32, kind="ExternalOutput").ap()
    gnn_kernel(nc, a, out)
    return _run(nc, [arrays], core_ids=[0]).results[0]["out_0_dram"]
```
